# Optimizing a Trainium2 kernel written in Bass

```python
import numpy as np
import jax
import jax.numpy as jnp

def _softmax(x, axis=-1):
    return jax.nn.softmax(x, axis=axis)

def _gelu(x):
    return jax.nn.gelu(x, approximate=True)

def _silu(x):
    return jax.nn.silu(x)

def _sigmoid(x):
    return jax.nn.sigmoid(x)

def _layernorm(x, axis=-1, eps=1e-05):
    m = jnp.mean(x, axis=axis, keepdims=True)
    v = jnp.var(x, axis=axis, keepdims=True)
    return (x - m) / jnp.sqrt(v + eps)

def _scatter_add(tgt, idx, src, axis=0):
    return tgt.at[idx].add(src)

def _segment_sum(src, seg, n):
    return jax.ops.segment_sum(src, seg, n)
kernel_name = 'mk_seq_postln_d1_jaxref_r8_86fc22'

def setup_inputs(seed: int=0):
    np.random.seed(seed)
    _w = jnp.asarray

    def _L0_attn_setup():
        import jax, jax.numpy as jnp
        import numpy as np
        D_MODEL = 128
        NUM_HEADS = 16
        HEAD_DIM = D_MODEL // NUM_HEADS
        MAX_SEQ_LEN = 256

        def _rope_tables(seq_len, head_dim):
            inv_freq = 1.0 / 10000.0 ** (jnp.arange(0, head_dim, 2, dtype=jnp.float32) / head_dim)
            pos = jnp.arange(seq_len, dtype=jnp.float32)
            freqs = jnp.einsum('i,j->ij', pos, inv_freq)
            return (jnp.cos(freqs), jnp.sin(freqs))

        def _apply_rope(x, cos_half, sin_half):
            x_even = x[..., ::2]
            x_odd = x[..., 1::2]
            rot_even = x_even * cos_half - x_odd * sin_half
            rot_odd = x_even * sin_half + x_odd * cos_half
            return jnp.stack([rot_even, rot_odd], axis=-1).reshape(x.shape)
        key = jax.random.key(seed)
        ks = jax.random.split(key, 9)
        B, S = (2, 256)
        glorot = lambda k: jax.random.normal(k, (D_MODEL, D_MODEL), dtype=jnp.float32) * (1.0 / np.sqrt(D_MODEL))
        return {'x': jax.random.normal(ks[0], (B, S, D_MODEL), dtype=jnp.float32), 'wq': glorot(ks[1]), 'bq': jnp.zeros((D_MODEL,), jnp.float32), 'wk': glorot(ks[2]), 'bk': jnp.zeros((D_MODEL,), jnp.float32), 'wv': glorot(ks[3]), 'bv': jnp.zeros((D_MODEL,), jnp.float32), 'wo': glorot(ks[4]), 'bo': jnp.zeros((D_MODEL,), jnp.float32)}
    _L0_attn_in = _L0_attn_setup()

    def _L0_ffn_setup():
        import jax, jax.numpy as jnp
        import numpy as np
        E = 8
        D = 128
        H = 256
        TOP_K = 2
        key = jax.random.key(seed)
        k_x, k_g, k_w1, k_w2 = jax.random.split(key, 4)
        B, S = (4, 256)
        inp = {'input': jax.random.normal(k_x, (B, S, D), dtype=jnp.float32), 'Wg': jax.random.normal(k_g, (D, E), dtype=jnp.float32) * 0.02, 'W1': jax.random.normal(k_w1, (E, D, H), dtype=jnp.float32) * 0.02, 'b1': jnp.zeros((E, H), dtype=jnp.float32), 'W2': jax.random.normal(k_w2, (E, H, D), dtype=jnp.float32) * 0.02, 'b2': jnp.zeros((E, D), dtype=jnp.float32)}
        return inp
    _L0_ffn_in = _L0_ffn_setup()
    _d = {'L0_attn_x': _L0_attn_in['x'], 'L0_attn_wq': _L0_attn_in['wq'], 'L0_attn_bq': _L0_attn_in['bq'], 'L0_attn_wk': _L0_attn_in['wk'], 'L0_attn_bk': _L0_attn_in['bk'], 'L0_attn_wv': _L0_attn_in['wv'], 'L0_attn_bv': _L0_attn_in['bv'], 'L0_attn_wo': _L0_attn_in['wo'], 'L0_attn_bo': _L0_attn_in['bo'], 'L0_ffn_Wg': _L0_ffn_in['Wg'], 'L0_ffn_W1': _L0_ffn_in['W1'], 'L0_ffn_b1': _L0_ffn_in['b1'], 'L0_ffn_W2': _L0_ffn_in['W2'], 'L0_ffn_b2': _L0_ffn_in['b2']}
    _x0 = _d['L0_attn_x']
    _d['L0_attn_x'] = jax.random.normal(jax.random.fold_in(jax.random.key(seed), 1), (16, 256, 128), dtype=_x0.dtype)
    del _x0
    return _d

def reference(L0_attn_x, L0_attn_wq, L0_attn_bq, L0_attn_wk, L0_attn_bk, L0_attn_wv, L0_attn_bv, L0_attn_wo, L0_attn_bo, L0_ffn_Wg, L0_ffn_W1, L0_ffn_b1, L0_ffn_W2, L0_ffn_b2):

    def _L0_attn_ref(x, wq, bq, wk, bk, wv, bv, wo, bo):
        import jax, jax.numpy as jnp
        import numpy as np
        D_MODEL = 128
        NUM_HEADS = 16
        HEAD_DIM = D_MODEL // NUM_HEADS
        MAX_SEQ_LEN = 256

        def _rope_tables(seq_len, head_dim):
            inv_freq = 1.0 / 10000.0 ** (jnp.arange(0, head_dim, 2, dtype=jnp.float32) / head_dim)
            pos = jnp.arange(seq_len, dtype=jnp.float32)
            freqs = jnp.einsum('i,j->ij', pos, inv_freq)
            return (jnp.cos(freqs), jnp.sin(freqs))

        def _apply_rope(x, cos_half, sin_half):
            x_even = x[..., ::2]
            x_odd = x[..., 1::2]
            rot_even = x_even * cos_half - x_odd * sin_half
            rot_odd = x_even * sin_half + x_odd * cos_half
            return jnp.stack([rot_even, rot_odd], axis=-1).reshape(x.shape)
        B, S, _ = x.shape
        q = (x @ wq + bq).reshape(B, S, NUM_HEADS, HEAD_DIM)
        k = (x @ wk + bk).reshape(B, S, NUM_HEADS, HEAD_DIM)
        v = (x @ wv + bv).reshape(B, S, NUM_HEADS, HEAD_DIM)
        cos, sin = _rope_tables(S, HEAD_DIM)
        cos = cos[None, :, None, :]
        sin = sin[None, :, None, :]
        q = _apply_rope(q, cos, sin)
        k = _apply_rope(k, cos, sin)
        q = q.transpose(0, 2, 1, 3)
        k = k.transpose(0, 2, 1, 3)
        v = v.transpose(0, 2, 1, 3)
        scores = jnp.einsum('bhqd,bhkd->bhqk', q, k) / jnp.sqrt(jnp.float32(HEAD_DIM))
        causal = jnp.where(jnp.tril(jnp.ones((S, S), jnp.float32)) == 0, -1000000000.0, 0.0)
        scores = scores + causal
        attn = jax.nn.softmax(scores, axis=-1)
        out = jnp.einsum('bhqk,bhkd->bhqd', attn, v)
        out = out.transpose(0, 2, 1, 3).reshape(B, S, D_MODEL)
        return out @ wo + bo

    def _L0_ffn_ref(input, Wg, W1, b1, W2, b2):
        import jax, jax.numpy as jnp
        import numpy as np
        E = 8
        D = 128
        H = 256
        TOP_K = 2
        logits = jnp.einsum('bsd,de->bse', input, Wg)
        probs = jax.nn.softmax(logits, axis=-1)
        top_vals, top_idx = jax.lax.top_k(probs, TOP_K)
        top_vals = top_vals / jnp.sum(top_vals, axis=-1, keepdims=True)
        onehot = jax.nn.one_hot(top_idx, E, dtype=input.dtype)
        mask = jnp.sum(onehot, axis=2)
        scores = jnp.sum(onehot * top_vals[..., None], axis=2)
        xm = input[None] * jnp.moveaxis(mask, -1, 0)[..., None]
        h = jnp.einsum('ebsd,edh->ebsh', xm, W1) + b1[:, None, None, :]
        h = jax.nn.relu(h)
        y = jnp.einsum('ebsh,ehd->ebsd', h, W2) + b2[:, None, None, :]
        out = jnp.sum(y * jnp.moveaxis(scores, -1, 0)[..., None], axis=0)
        return out
    x = L0_attn_x
    x = _layernorm(x + _L0_attn_ref(x, L0_attn_wq, L0_attn_bq, L0_attn_wk, L0_attn_bk, L0_attn_wv, L0_attn_bv, L0_attn_wo, L0_attn_bo), axis=-1)
    x = _layernorm(x + _L0_ffn_ref(x, L0_ffn_Wg, L0_ffn_W1, L0_ffn_b1, L0_ffn_W2, L0_ffn_b2), axis=-1)
    return x

_drawn_inputs = setup_inputs


def setup_inputs(seed=0):
    import zlib

    import numpy as np

    out = dict(_drawn_inputs(seed))
    spreads = {'L0_attn_bq': (0.0, 0.413),
     'L0_attn_bk': (0.0, 0.52),
     'L0_attn_bv': (0.0, 0.1),
     'L0_attn_bo': (0.0, 0.1),
     'L0_ffn_b1': (0.0, 0.533),
     'L0_ffn_b2': (0.0, 0.1)}
    factors = {}
    for name, (base, spread) in spreads.items():
        noise = np.random.default_rng([zlib.crc32(name.encode()), seed]).standard_normal(out[name].shape)
        drawn = base * np.exp(spread * noise) if base else spread * noise
        out[name] = jnp.asarray(drawn.astype(out[name].dtype))
    for name, factor in factors.items():
        out[name] = (out[name] * factor).astype(out[name].dtype)
    return out
```

```python
from contextlib import ExitStack

import numpy as np

import concourse.bass as bass
from concourse import mybir

F32 = mybir.dt.float32
F32R = mybir.dt.float32r
U32 = mybir.dt.uint32
ALU = mybir.AluOpType
ACT = mybir.ActivationFunctionType

P = 128
BATCHES, SEQ, D = 16, 256, 128
HEADS = 16
HD = D // HEADS
TILES = SEQ // P
ROWS = 32
GROUP = P // ROWS
GROUPS = HEADS // GROUP
MAX_ROW = 3 * HD
EXPERTS, HIDDEN = 8, 256
HT = HIDDEN // P
EPS = 1e-5
SCALE = float(1.0 / np.sqrt(np.float32(HD)))
MASKED = -1e9 / SCALE
CAUSAL = SEQ + P
BANK = 512

PV_BEATS = (6, 10, 14, 18)
O_BEATS = (11, 19)
QK_BEATS = (9, 10, 11, 12)
HIDDEN_BEATS = tuple(1 + 3 * e for e in range(EXPERTS))
EXPERT_BEATS = tuple(7 + 3 * e for e in range(EXPERTS))

PREP, DONE, RT, LN = 7, 11, 13, 5
TABLES = 16 * 14


class Batch:

    def __init__(self, pair, parity):
        self.pair, self.parity = pair, parity

    @property
    def n(self):
        return self.pair * 2 + self.parity

    def shift(self, k):
        m = self.parity + k
        return Batch(self.pair + m // 2, m % 2)

    def at_start(self, k=0):
        return isinstance(self.pair, int) and self.n <= k


def layer(nc, x, wq, bq, wk, bk, wv, bv, wo, bo, wg, w1, b1, w2, b2, rope, mask, ident, pick, out):
    with ExitStack() as ctx:
        def sb(name, shape, dt=F32):
            return ctx.enter_context(nc.sbuf_tensor(name, shape, dt))

        def bank(name):
            return ctx.enter_context(nc.psum_tensor(name, [P, BANK], F32))

        def sem(name):
            return ctx.enter_context(nc.semaphore(name))

        wqkv = sb("wqkv", [P, 3 * D])
        bqkv = sb("bqkv", [P, 3 * D])
        wo_sb = sb("wo_sb", [P, D])
        bo_sb = sb("bo_sb", [P, D])
        wg_sb = sb("wg_sb", [P, EXPERTS])
        w1_sb = sb("w1_sb", [P, EXPERTS, HIDDEN])
        w2_sb = sb("w2_sb", [P, EXPERTS * HT, D])
        b1_rows = sb("b1_rows", [EXPERTS * HT, P])
        b1_cols = sb("b1_cols", [P, EXPERTS * HT])
        b2_sb = sb("b2_sb", [2 * EXPERTS, D])
        rope_sb = sb("rope_sb", [P, 2, TILES, HD])
        mask_sb = sb("mask_sb", [P, SEQ])
        ident_sb = sb("ident_sb", [P, P])
        pick_raw = sb("pick_raw", [2 * EXPERTS, EXPERTS, P])
        pick_sb = sb("pick_sb", [2 * EXPERTS, EXPERTS, P], F32R)
        iota = sb("iota", [P, EXPERTS])
        neg_half = sb("neg_half", [P, TILES])

        x_tok = sb("x_tok", [P, 2, TILES, D])
        x_bo = sb("x_bo", [P, 2, TILES, D])
        xT = sb("xT", [P, SEQ])
        qk = sb("qk", [P, TILES, 2 * HEADS, HD])
        rope_cos = sb("rope_cos", [P, TILES, 2 * HEADS, HD])
        rope_sin = sb("rope_sin", [P, TILES, 2 * HEADS, HD])
        rot = sb("rot", [P, 2, TILES, HEADS, HD])
        split = sb("split", [P, 2, TILES, HEADS, ROWS])
        kT = sb("kT", [P, 2, GROUPS, SEQ], F32R)
        qT_max = sb("qT_max", [P, GROUPS, SEQ], F32R)
        qT = sb("qT", [P, GROUPS, SEQ], F32R)
        v_aug = sb("v_aug", [P, 2, TILES, HEADS, ROWS])
        junk = sb("junk", [P, 2, TILES, SEQ])
        row_max = sb("row_max", [P, TILES, HEADS])
        probs = sb("probs", [P, HEADS, CAUSAL])
        oT = sb("oT", [P, GROUPS, SEQ])
        recip = sb("recip", [P, TILES, HEADS])
        attn = sb("attn", [P, TILES, HEADS, HD])
        attnT = sb("attnT", [P, SEQ])
        z1 = sb("z1", [P, TILES, D])
        stats1 = sb("stats1", [P, TILES, 6])
        mv1 = sb("mv1", [P, TILES, 2])
        var1 = sb("var1", [P, TILES])
        rstd1 = sb("rstd1", [P, TILES])
        x1 = sb("x1", [P, 2, TILES, D])
        x1T = sb("x1T", [P, 2, SEQ])
        logits = sb("logits", [P, TILES, EXPERTS])
        top_logits = sb("top_logits", [P, TILES, 8])
        neg_top = sb("neg_top", [P, TILES])
        expd = sb("expd", [P, TILES, EXPERTS])
        top = sb("top", [P, TILES, 8])
        top_at = sb("top_at", [P, TILES, 8], U32)
        top_atf = sb("top_atf", [P, TILES, 2])
        top_sum = sb("top_sum", [P, TILES])
        top_inv = sb("top_inv", [P, TILES])
        hot = sb("hot", [P, 2, TILES, EXPERTS])
        hot_sum = sb("hot_sum", [P, TILES, EXPERTS])
        score = sb("score", [P, TILES, EXPERTS])
        score_split = sb("score_split", [P, TILES, 2 * EXPERTS])
        scoreT = sb("scoreT", [2 * EXPERTS, SEQ], F32R)
        score_all = sb("score_all", [P, 2, EXPERTS, SEQ])
        hid = sb("hid", [P, 2, HT, SEQ])
        hid_scaled = sb("hid_scaled", [P, 2, HT, SEQ])
        yT = sb("yT", [P, SEQ])
        z2 = sb("z2", [P, TILES, D])
        stats2 = sb("stats2", [P, TILES, 6])
        mv2 = sb("mv2", [P, TILES, 2])
        var2 = sb("var2", [P, TILES])
        rstd2 = sb("rstd2", [P, TILES])
        out_tok = sb("out_tok", [P, 2, TILES, D])

        ps_score = [bank("ps_score0"), bank("ps_score1")]
        ps_pv = bank("ps_pv")
        ps_hid = [bank("ps_hid0"), bank("ps_hid1")]
        ps_y = bank("ps_y")
        ps_prep = bank("ps_prep")
        ps_done = bank("ps_done")

        tables_loaded = sem("tables_loaded")
        w_loaded = sem("w_loaded")
        zeroed = sem("zeroed")
        padded = sem("padded")
        b1_turned = sem("b1_turned")
        setup_done = sem("setup_done")
        x_loaded = [sem("x_loaded0"), sem("x_loaded1")]
        x_bo_ready = sem("x_bo_ready")
        prep_full = sem("prep_full")
        prep_read = sem("prep_read")
        rope_terms = sem("rope_terms")
        roped = sem("roped")
        high_ready = sem("high_ready")
        split_ready = sem("split_ready")
        max_full = sem("max_full")
        max_read = sem("max_read")
        neg_max_ready = sem("neg_max_ready")
        qT_full = sem("qT_full")
        qT_read = sem("qT_read")
        scores_full = sem("scores_full")
        exp_done = sem("exp_done")
        cut = sem("cut")
        pv_full = sem("pv_full")
        pv_read = sem("pv_read")
        done_full = sem("done_full")
        done_read = sem("done_read")
        recip_ready = sem("recip_ready")
        ln1_step = sem("ln1_step")
        rstd1_ready = sem("rstd1_ready")
        x1_ready = sem("x1_ready")
        route_step = sem("route_step")
        route_split = sem("route_split")
        route_exp = sem("route_exp")
        hid_full = sem("hid_full")
        hid_ready = sem("hid_ready")
        hid_scaled_ready = sem("hid_scaled_ready")
        expert_added = sem("expert_added")
        y_read = sem("y_read")
        emit_full = sem("emit_full")
        emit_read = sem("emit_read")
        ln2_step = sem("ln2_step")
        rstd2_ready = sem("rstd2_ready")
        out_ready = sem("out_ready")
        stored = [sem("stored0"), sem("stored1")]

        def schedule(eng, start, frame):
            start()
            frame(Batch(0, 0), {"prepare", "maxima", "attend", "finish"})
            frame(Batch(0, 1), {"prepare", "maxima", "attend", "finish", "experts"})
            every = {"prepare", "maxima", "attend", "finish", "experts", "emit"}
            with eng.Fori(1, BATCHES // 2 - 1) as pair:
                for parity in range(2):
                    frame(Batch(pair, parity), every)
            last = BATCHES // 2 - 1
            frame(Batch(last, 0), every)
            frame(Batch(last, 1), every - {"prepare", "maxima"})
            frame(Batch(last + 1, 0), {"experts", "emit"})
            frame(Batch(last + 1, 1), {"emit"})

        def value(eng, count):
            return count if isinstance(count, int) else eng.to_reg(count)

        def wait_apart(eng, semaphore, count):
            count = value(eng, count)
            eng.wait_ge(tables_loaded, TABLES)
            eng.wait_ge(semaphore, count)

        block = ctx.enter_context(nc.Block())

        @block.sync
        def _(sp):
            def load(b):
                src = x[bass.ds(b.n, 1)].rearrange("a (t p) d -> p (a t) d", p=P)
                sp.dma_start(x_tok[:, b.parity], src).then_inc(x_loaded[b.parity], 16)

            def start():
                load(Batch(0, 0))
                for i, (w, b) in enumerate(((wq, bq), (wk, bk), (wv, bv))):
                    sp.dma_start(wqkv[:, i * D:(i + 1) * D], w).then_inc(tables_loaded, 16)
                    sp.dma_start(bqkv[:, i * D:(i + 1) * D], b.partition_broadcast(P)).then_inc(tables_loaded, 16)
                sp.dma_start(ident_sb[:], ident).then_inc(tables_loaded, 16)
                sp.dma_start(rope_sb[:], rope).then_inc(tables_loaded, 16)
                sp.dma_start(mask_sb[:], mask).then_inc(tables_loaded, 16)
                sp.dma_start(bo_sb[:], bo.partition_broadcast(P)).then_inc(tables_loaded, 16)
                sp.dma_start(wo_sb[:], wo).then_inc(tables_loaded, 16)
                sp.dma_start(wg_sb[:], wg).then_inc(tables_loaded, 16)
                sp.dma_start(b1_rows[:], b1.rearrange("e (t p) -> (e t) p", p=P)).then_inc(tables_loaded, 16)
                sp.dma_start(pick_raw[:], pick).then_inc(tables_loaded, 16)
                load(Batch(0, 1))
                sp.dma_start(w1_sb[:], w1.rearrange("e d h -> d e h")).then_inc(w_loaded, 16)
                sp.dma_start(w2_sb[:], w2.rearrange("e (t p) d -> p (e t) d", p=P)).then_inc(w_loaded, 16)
                for i in range(2):
                    sp.dma_start(b2_sb[i * EXPERTS:(i + 1) * EXPERTS, :], b2).then_inc(w_loaded, 16)

            def frame(b, stages):
                if "prepare" in stages and not (isinstance(b.pair, int) and b.pair >= BATCHES // 2 - 1):
                    turned, added = value(sp, b.n * PREP + 1), value(sp, b.n + 1)
                    sp.wait_ge(prep_full, turned)
                    sp.wait_ge(x_bo_ready, added)
                    load(b.shift(2))
                if "emit" in stages:
                    e = b.shift(-2)
                    sp.wait_ge(out_ready, e.n * TILES + TILES)
                    dst = out[bass.ds(e.n, 1)].rearrange("a (t p) d -> p (a t) d", p=P)
                    sp.dma_start(dst, out_tok[:, e.parity]).then_inc(stored[e.parity], 16)

            schedule(sp, start, frame)
            for s in stored:
                sp.wait_ge(s, 16 * BATCHES // 2)

        @block.tensor
        def _(pe):
            def turn(dst, src, n=P):
                return pe.transpose(dst, src, ident_sb[:n, :n])

            def prep_fill(b, k):
                if k:
                    pe.wait_ge(prep_read, b.n * PREP + k)
                elif not b.at_start():
                    pe.wait_ge(qT_read, b.n * 2)

            def turn_x(b):
                prep_fill(b, 0)
                pe.wait_ge(x_loaded[b.parity], b.pair * 16 + 16)
                for t in range(TILES):
                    last = turn(ps_prep[:, t * P:(t + 1) * P], x_tok[:, b.parity, t, :])
                last.then_inc(prep_full, 1)

            def project(b, t):
                prep_fill(b, 1 + t)
                pe.matmul(ps_prep[:, 0:3 * D], xT[:, t * P:(t + 1) * P], wqkv[:], start=True,
                          stop=True).then_inc(prep_full, 1)

            def turn_split(which, half):
                for g in range(2):
                    for t in range(TILES):
                        src = split[:, which, t, (2 * half + g) * GROUP:(2 * half + g + 1) * GROUP, :]
                        last = turn(ps_prep[:, g * SEQ + t * P:g * SEQ + (t + 1) * P],
                                    src.rearrange("p h r -> p (h r)"))
                return last

            def turn_qk(b, i):
                prep_fill(b, 3 + i)
                if i == 0:
                    pe.wait_ge(split_ready, b.n * 2 + 2)
                turn_split(1 - i // 2, i % 2).then_inc(prep_full, 1)

            def turn_queries(b, half):
                if half == 0:
                    pe.wait_ge(neg_max_ready, b.n + 1)
                    pe.wait_ge(prep_read, b.n * PREP + PREP)
                else:
                    pe.wait_ge(qT_read, b.n * 2 + 1)
                turn_split(0, half).then_inc(qT_full, 1)

            def max_scores(b, h):
                g, r = h // GROUP, h % GROUP * ROWS
                if h >= 2:
                    pe.wait_ge(max_read, b.n * HEADS + h - 1)
                elif h == 0:
                    pe.wait_ge(prep_read, b.n * PREP + PREP)
                if h < 2 and not b.at_start():
                    pe.wait_ge(exp_done, b.n * HEADS - 1 + h)
                for t in range(TILES):
                    last = pe.matmul(ps_score[h % 2][:, t * SEQ:(t + 1) * SEQ],
                                     qT_max[r:r + MAX_ROW, g, t * P:(t + 1) * P],
                                     kT[r:r + MAX_ROW, b.parity, g, :], start=True, stop=True)
                last.then_inc(max_full, 1)

            def scores(b, h):
                g, r = h // GROUP, h % GROUP * ROWS
                if h == 0:
                    pe.wait_ge(qT_read, b.n * 2 + 2)
                if h >= 2:
                    pe.wait_ge(exp_done, b.n * HEADS + h - 1)
                else:
                    pe.wait_ge(max_read, b.n * HEADS + HEADS - 1 + h)
                for i, t in enumerate(reversed(range(TILES))):
                    last = pe.matmul(ps_score[h % 2][:, i * SEQ:(i + 1) * SEQ],
                                     kT[r:r + ROWS, b.parity, g, t * P:(t + 1) * P],
                                     qT[r:r + ROWS, g, :], start=True, stop=True)
                last.then_inc(scores_full, 1)

            def times_v(b, g):
                pe.wait_ge(cut, b.n * (HEADS // 2) + 2 * g + 2)
                if g == 2:
                    pe.wait_ge(pv_read, b.n * 2 + 1)
                elif g == 0 and not b.at_start():
                    pe.wait_ge(pv_read, b.n * 2)
                for j in range(GROUP):
                    h, c = g * GROUP + j, g % 2 * SEQ
                    dst = ps_pv[j * ROWS:(j + 1) * ROWS, :]
                    pe.matmul(dst[:, c:c + SEQ], v_aug[:, b.parity, 0, h, :], probs[:, h, P:CAUSAL],
                              start=True, stop=False)
                    last = pe.matmul(dst[:, c + P:c + SEQ], v_aug[:, b.parity, 1, h, :], probs[:, h, 0:P],
                                     start=False, stop=True)
                if g % 2:
                    last.then_inc(pv_full, 1)

            def done_fill(b, k):
                if k:
                    pe.wait_ge(done_read, b.n * DONE + k)
                elif not b.at_start(1):
                    pe.wait_ge(emit_read, b.n - 1)

            def turn_o(b, t):
                done_fill(b, t)
                if t == 0:
                    pe.wait_ge(pv_read, b.n * 2 + 2)
                for g in range(GROUPS):
                    last = turn(ps_done[:, g * P:(g + 1) * P], oT[:, g, t * P:(t + 1) * P])
                last.then_inc(done_full, 1)

            def turn_attn(b):
                done_fill(b, 2)
                for t in range(TILES):
                    last = turn(ps_done[:, t * P:(t + 1) * P], attn[:, t].rearrange("p h d -> p (h d)"))
                last.then_inc(done_full, 1)

            def project_o(b):
                done_fill(b, 3)
                for t in range(TILES):
                    last = pe.matmul(ps_done[:, t * P:(t + 1) * P], attnT[:, t * P:(t + 1) * P], wo_sb[:],
                                     start=True, stop=True)
                last.then_inc(done_full, 1)

            def turn_x1(b):
                done_fill(b, 4)
                pe.wait_ge(x1_ready, b.n * TILES + TILES)
                for t in range(TILES):
                    last = turn(ps_done[:, t * P:(t + 1) * P], x1[:, b.parity, t, :])
                last.then_inc(done_full, 1)

            def route(b):
                done_fill(b, 5)
                for t in range(TILES):
                    last = pe.matmul(ps_done[:, t * EXPERTS:(t + 1) * EXPERTS],
                                     x1T[:, b.parity, t * P:(t + 1) * P], wg_sb[:], start=True, stop=True)
                last.then_inc(done_full, 1)

            def turn_score(b):
                done_fill(b, 6)
                pe.wait_ge(route_step, b.n * RT + RT)
                for t in range(TILES):
                    last = turn(ps_done[0:2 * EXPERTS, t * P:(t + 1) * P], score_split[:, t, :])
                last.then_inc(done_full, 1)

            def spread_score(b, i):
                done_fill(b, 7 + i)
                if b.at_start() and i == 0:
                    pe.wait_ge(setup_done, 2)
                for j in range(2):
                    last = pe.matmul(ps_done[:, j * SEQ:(j + 1) * SEQ], pick_sb[:, 2 * i + j, :], scoreT[:],
                                     start=True, stop=True)
                last.then_inc(done_full, 1)

            def hidden(b, e):
                if e >= 2 or not b.at_start():
                    pe.wait_ge(hid_ready, b.n * EXPERTS + e - 1)
                if b.at_start() and e == 0:
                    pe.wait_ge(w_loaded, 64)
                for t in range(HT):
                    last = pe.matmul(ps_hid[e % 2][:, t * SEQ:(t + 1) * SEQ],
                                     w1_sb[:, e, t * P:(t + 1) * P], x1T[:, b.parity, :],
                                     start=True, stop=True)
                last.then_inc(hid_full, 1)

            def add_expert(b, e):
                if e == 0:
                    if not b.at_start():
                        pe.wait_ge(y_read, b.n)
                    pe.matmul(ps_y[:, 0:SEQ], b2_sb[:], scoreT[:].bitcast(F32), start=True, stop=False)
                pe.wait_ge(hid_scaled_ready, b.n * EXPERTS + e + 1)
                for t in range(HT):
                    last = pe.matmul(ps_y[:, 0:SEQ], w2_sb[:, e * HT + t, :], hid_scaled[:, e % 2, t, :],
                                     start=False, stop=(e == EXPERTS - 1 and t == HT - 1))
                last.then_inc(expert_added, 1)

            def turn_y(b):
                pe.wait_ge(y_read, b.n + 1)
                last_finish = BATCHES if b.at_start(BATCHES) and b.n == BATCHES - 1 else b.n + 2
                pe.wait_ge(done_read, last_finish * DONE)
                for t in range(TILES):
                    last = turn(ps_done[:, t * P:(t + 1) * P], yT[:, t * P:(t + 1) * P])
                last.then_inc(emit_full, 1)

            def prepare_and_maxima(b):
                turn_x(b)
                for t in range(TILES):
                    project(b, t)
                for i in range(4):
                    turn_qk(b, i)
                for h in range(HEADS):
                    max_scores(b, h)

            def start():
                pe.wait_ge(tables_loaded, TABLES)
                turn(ps_done[:, 0:EXPERTS * HT], b1_rows[:], EXPERTS * HT).then_inc(b1_turned, 1)
                pe.wait_ge(setup_done, 1)
                prepare_and_maxima(Batch(0, 0))

            def frame(b, stages):
                nxt, prev, old = b.shift(1), b.shift(-1), b.shift(-2)
                if "attend" in stages:
                    for half in range(2):
                        turn_queries(b, half)
                for i in range(2 * HEADS):
                    if "attend" in stages:
                        if i < HEADS:
                            scores(b, i)
                        if i in PV_BEATS:
                            times_v(b, PV_BEATS.index(i))
                    if "maxima" in stages and i >= HEADS:
                        max_scores(nxt, i - HEADS)
                    if "prepare" in stages:
                        if i == 0:
                            turn_x(nxt)
                        if i in (2, 3):
                            project(nxt, i - 2)
                        if i in QK_BEATS:
                            turn_qk(nxt, QK_BEATS.index(i))
                    if "emit" in stages and i == 1:
                        turn_y(old)
                    if "experts" in stages:
                        if i in HIDDEN_BEATS:
                            hidden(prev, HIDDEN_BEATS.index(i))
                        if i in EXPERT_BEATS:
                            add_expert(prev, EXPERT_BEATS.index(i))
                    if "finish" in stages:
                        if i in (20, 21):
                            turn_o(b, i - 20)
                        if i == 22:
                            turn_attn(b)
                        if i == 23:
                            project_o(b)
                        if i == 26:
                            turn_x1(b)
                        if i == 27:
                            route(b)
                        if i == 30:
                            turn_score(b)
                        if i == 31:
                            for k in range(4):
                                spread_score(b, k)

            schedule(pe, start, frame)

        @block.scalar
        def _(act):
            def copy_xT(b):
                act.wait_ge(prep_full, b.n * PREP + 1)
                act.activation(xT[:], ps_prep[:, 0:SEQ], ACT.Copy).then_inc(prep_read, 1)

            def exponent(b, h):
                act.wait_ge(scores_full, b.n * HEADS + h + 1)
                act.activation(probs[:, h, :], ps_score[h % 2][:, P:P + CAUSAL], ACT.Exp,
                               scale=SCALE).then_inc(exp_done, 1)

            def copy_o(b, half):
                act.wait_ge(pv_full, b.n * 2 + half + 1)
                act.activation(oT[:, 2 * half:2 * half + 2, :].rearrange("p g s -> p (g s)"), ps_pv[:],
                               ACT.Copy).then_inc(pv_read, 1)

            def copy_done(b, k, dst, n):
                act.wait_ge(done_full, b.n * DONE + k + 1)
                act.activation(dst, ps_done[:, 0:n], ACT.Copy).then_inc(done_read, 1)

            def route_exponent(b):
                act.wait_ge(route_step, b.n * RT + 3)
                for t in range(TILES):
                    act.activation(expd[:, t, :], logits[:, t, :], ACT.Exp,
                                   bias=neg_top[:, t:t + 1]).then_inc(route_exp, 1)

            def relu(b, e):
                if e >= 2 or not b.at_start():
                    act.wait_ge(hid_scaled_ready, b.n * EXPERTS + e - 1)
                act.wait_ge(hid_full, b.n * EXPERTS + e + 1)
                for t in range(HT):
                    last = act.activation(hid[:, e % 2, t, :], ps_hid[e % 2][:, t * SEQ:(t + 1) * SEQ], ACT.Relu,
                                          bias=b1_cols[:, e * HT + t:e * HT + t + 1])
                last.then_inc(hid_ready, 1)

            def copy_y(b):
                act.wait_ge(expert_added, b.n * EXPERTS + EXPERTS)
                act.activation(yT[:], ps_y[:, 0:SEQ], ACT.Copy).then_inc(y_read, 1)

            def start():
                copy_xT(Batch(0, 0))
                act.wait_ge(setup_done, 2)

            def frame(b, stages):
                nxt, prev, old = b.shift(1), b.shift(-1), b.shift(-2)
                for i in range(2 * HEADS):
                    if "attend" in stages:
                        if i < HEADS:
                            exponent(b, i)
                        if i in O_BEATS:
                            copy_o(b, O_BEATS.index(i))
                    if "emit" in stages and i == 0:
                        copy_y(old)
                    if "prepare" in stages and i == 0:
                        copy_xT(nxt)
                    if "experts" in stages and i - 1 in HIDDEN_BEATS:
                        relu(prev, HIDDEN_BEATS.index(i - 1))
                    if "finish" in stages:
                        if i == 22:
                            copy_done(b, 2, attnT[:], SEQ)
                        if i == 26:
                            copy_done(b, 4, x1T[:, b.parity, :], SEQ)
                        if i == 28:
                            route_exponent(b)
                        if i == 31:
                            for k in (0, 2):
                                copy_done(b, 7 + k, score_all[:, b.parity, 2 * k:2 * k + 2, :]
                                          .rearrange("p e s -> p (e s)"), 2 * SEQ)

            schedule(act, start, frame)

        @block.vector
        def _(dve):
            def bias_qkv(b, t):
                dve.wait_ge(prep_full, b.n * PREP + 2 + t)
                if not b.at_start():
                    dve.wait_ge(roped, b.n * TILES)
                dve.tensor_tensor(qk[:, t].rearrange("p h d -> p (h d)"), ps_prep[:, 0:2 * D],
                                  bqkv[:, 0:2 * D], ALU.add)
                dve.tensor_tensor(v_aug[:, b.parity, t, :, 0:HD],
                                  ps_prep[:, 2 * D:3 * D].rearrange("p (h d) -> p h d", d=HD),
                                  bqkv[:, 2 * D:3 * D].rearrange("p (h d) -> p h d", d=HD),
                                  ALU.add).then_inc(prep_read, 1)

            def slots(which, first, step, n):
                rows = split[:, which].rearrange("p t h (s d) -> p (t h) s d", d=HD)
                return rows[:, :, first:first + step * (n - 1) + 1:step, :].bitcast(F32R)

            def split_qk(b):
                dve.wait_ge(roped, b.n * TILES + TILES)
                if not b.at_start():
                    dve.wait_ge(qT_full, b.n * 2)
                src = [rot[:, w].rearrange("p t h d -> p (t h) d") for w in range(2)]
                for w, step in ((0, 1), (1, 2)):
                    dve.tensor_copy(slots(w, 0, step, 2),
                                    src[w].unsqueeze(2).to_broadcast([P, TILES * HEADS, 2, HD])
                                    ).then_inc(high_ready, 1)
                for w, low in ((0, 2), (1, 1)):
                    dve.wait_ge(high_ready, b.n * 2 + w + 1)
                    dve.tensor_tensor(slots(w, low, 1, 1)[:, :, 0, :], src[w],
                                      slots(w, 0, 1, 1)[:, :, 0, :].bitcast(F32),
                                      ALU.subtract).then_inc(split_ready, 1)

            def copy_qk(b, i):
                dve.wait_ge(prep_full, b.n * PREP + 4 + i)
                half = 2 * (i % 2)
                dst = (kT[:, b.parity] if i < 2 else qT_max)[:, half:half + 2, :]
                dve.tensor_copy(dst.rearrange("p g s -> p (g s)"), ps_prep[:]).then_inc(prep_read, 1)

            def copy_queries(b, half):
                dve.wait_ge(qT_full, b.n * 2 + half + 1)
                dve.tensor_copy(qT[:, 2 * half:2 * half + 2, :].rearrange("p g s -> p (g s)"),
                                ps_prep[:]).then_inc(qT_read, 1)

            def take_max(b, h):
                wait_apart(dve, max_full, b.n * HEADS + h + 1)
                for t in range(TILES):
                    n = (t + 1) * P
                    last = dve.tensor_tensor_reduce(
                        out=junk[:, h % 2, t, 0:n], in0=ps_score[h % 2][:, t * SEQ:t * SEQ + n],
                        in1=mask_sb[:, SEQ - n:SEQ], scale=1.0, scalar=-3.0e38, op0=ALU.add, op1=ALU.max,
                        accum_out=row_max[:, t, h:h + 1])
                last.then_inc(max_read, 1)

            def negate_max(b):
                dve.wait_ge(max_read, b.n * HEADS + HEADS)
                dve.tensor_scalar(split[:, 0, :, :, MAX_ROW].bitcast(F32R), row_max[:], -1.0, None,
                                  ALU.mult).then_inc(neg_max_ready, 1)

            def normalise(b, t):
                dve.wait_ge(done_full, b.n * DONE + t + 1)
                o = ps_done[:].rearrange("p (h r) -> p h r", r=ROWS)
                dve.reciprocal(recip[:, t, :], o[:, :, HD]).then_inc(recip_ready, 1)
                dve.wait_ge(recip_ready, b.n * TILES + t + 1)
                dve.tensor_tensor(attn[:, t], o[:, :, 0:HD],
                                  recip[:, t, :].unsqueeze(2).to_broadcast([P, HEADS, HD]),
                                  ALU.mult).then_inc(done_read, 1)

            def moments(b, z, stats, mv, var, step):
                for t in range(TILES):
                    dve.bn_stats(stats[:, t, :], z[:, t, :]).then_inc(step, 1)
                for t in range(TILES):
                    wait_apart(dve, step, b.n * LN + t + 1)
                    dve.bn_aggr(mv[:, t, :], stats[:, t, :]).then_inc(step, 1)
                dve.wait_ge(step, b.n * LN + 4)
                dve.tensor_scalar(var[:], mv[:, :, 1], EPS, None, ALU.add).then_inc(step, 1)

            def residual1(b):
                dve.wait_ge(x_bo_ready, b.n + 1)
                dve.wait_ge(done_full, b.n * DONE + 4)
                dve.tensor_tensor(z1[:].rearrange("p t d -> p (t d)"), ps_done[:, 0:SEQ],
                                  x_bo[:, b.parity].rearrange("p t d -> p (t d)"), ALU.add).then_inc(done_read, 1)
                dve.wait_ge(done_read, b.n * DONE + 4)
                moments(b, z1, stats1, mv1, var1, ln1_step)

            def norm1(b):
                dve.wait_ge(rstd1_ready, b.n + 1)
                for t in range(TILES):
                    dve.tensor_scalar(x1[:, b.parity, t, :], z1[:, t, :], mv1[:, t, 0:1], rstd1[:, t:t + 1],
                                      ALU.subtract, ALU.mult).then_inc(x1_ready, 1)

            def route_logits(b):
                dve.wait_ge(done_full, b.n * DONE + 6)
                dve.tensor_copy(logits[:].rearrange("p t e -> p (t e)"),
                                ps_done[:, 0:TILES * EXPERTS]).then_inc(done_read, 1)
                wait_apart(dve, done_read, b.n * DONE + 6)
                for t in range(TILES):
                    dve.max(top_logits[:, t, :], logits[:, t, :]).then_inc(route_step, 1)
                dve.wait_ge(route_step, b.n * RT + 2)
                dve.tensor_scalar(neg_top[:], top_logits[:, :, 0], -1.0, None, ALU.mult).then_inc(route_step, 1)

            def route_scores(b):
                def after(k):
                    dve.wait_ge(route_step, b.n * RT + k)

                wait_apart(dve, route_exp, b.n * TILES + TILES)
                for t in range(TILES):
                    dve.max(top[:, t, :], expd[:, t, :]).then_inc(route_step, 1)
                wait_apart(dve, route_step, b.n * RT + 5)
                for t in range(TILES):
                    dve.max_index(top_at[:, t, :], top[:, t, :], expd[:, t, :]).then_inc(route_step, 1)
                dve.tensor_tensor(top_sum[:], top[:, :, 0], top[:, :, 1], ALU.add).then_inc(route_step, 1)
                after(7)
                dve.tensor_copy(top_atf[:], top_at[:, :, 0:2]).then_inc(route_step, 1)
                after(8)
                dve.reciprocal(top_inv[:], top_sum[:]).then_inc(route_step, 1)
                after(9)
                for t in range(TILES):
                    for k in range(2):
                        last = dve.tensor_scalar(hot[:, k, t, :], iota[:], top_atf[:, t, k:k + 1],
                                                 top[:, t, k:k + 1], ALU.is_equal, ALU.mult)
                last.then_inc(route_step, 1)
                after(11)
                dve.tensor_tensor(hot_sum[:], hot[:, 0], hot[:, 1], ALU.add).then_inc(route_split, 1)
                dve.wait_ge(route_split, b.n * 2 + 1)
                dve.tensor_tensor(score[:], hot_sum[:], top_inv[:].unsqueeze(2).to_broadcast([P, TILES, EXPERTS]),
                                  ALU.mult).then_inc(route_split, 1)
                dve.wait_ge(route_split, b.n * 2 + 2)
                high = score_split[:, :, 0:EXPERTS]
                dve.tensor_copy(high.bitcast(F32R), score[:]).then_inc(route_step, 1)
                after(12)
                dve.tensor_tensor(score_split[:, :, EXPERTS:2 * EXPERTS].bitcast(F32R), score[:], high,
                                  ALU.subtract).then_inc(route_step, 1)

            def copy_scoreT(b):
                dve.wait_ge(done_full, b.n * DONE + 7)
                dve.tensor_copy(scoreT[:], ps_done[0:2 * EXPERTS, 0:SEQ]).then_inc(done_read, 1)

            def copy_spread(b, k):
                dve.wait_ge(done_full, b.n * DONE + 8 + k)
                dve.tensor_copy(score_all[:, b.parity, 2 * k:2 * k + 2, :].rearrange("p e s -> p (e s)"),
                                ps_done[:]).then_inc(done_read, 1)

            def residual2(b):
                if not b.at_start():
                    dve.wait_ge(out_ready, b.n * TILES)
                dve.wait_ge(emit_full, b.n + 1)
                dve.tensor_tensor(z2[:].rearrange("p t d -> p (t d)"), ps_done[:, 0:SEQ],
                                  x1[:, b.parity].rearrange("p t d -> p (t d)"), ALU.add).then_inc(emit_read, 1)
                dve.wait_ge(emit_read, b.n + 1)
                moments(b, z2, stats2, mv2, var2, ln2_step)

            def norm2(b):
                if not b.at_start(1):
                    dve.wait_ge(stored[b.parity], b.pair * 16)
                dve.wait_ge(rstd2_ready, b.n + 1)
                for t in range(TILES):
                    dve.tensor_scalar(out_tok[:, b.parity, t, :], z2[:, t, :], mv2[:, t, 0:1], rstd2[:, t:t + 1],
                                      ALU.subtract, ALU.mult).then_inc(out_ready, 1)

            def start():
                dve.wait_ge(b1_turned, 1)
                dve.tensor_copy(b1_cols[:], ps_done[:, 0:EXPERTS * HT]).then_inc(setup_done, 1)
                dve.wait_ge(tables_loaded, TABLES)
                dve.tensor_copy(pick_sb[:], pick_raw[:]).then_inc(setup_done, 1)
                dve.wait_ge(padded, 5)
                b = Batch(0, 0)
                for t in range(TILES):
                    bias_qkv(b, t)
                split_qk(b)
                for i in range(4):
                    copy_qk(b, i)
                for h in range(HEADS):
                    take_max(b, h)
                negate_max(b)

            def frame(b, stages):
                nxt, old = b.shift(1), b.shift(-2)
                if "attend" in stages:
                    for half in range(2):
                        copy_queries(b, half)
                for i in range(2 * HEADS):
                    if "emit" in stages:
                        if i == 1:
                            residual2(old)
                        if i == 4:
                            norm2(old)
                    if "prepare" in stages:
                        if i in (2, 3):
                            bias_qkv(nxt, i - 2)
                        if i == QK_BEATS[0] - 1:
                            split_qk(nxt)
                        if i in QK_BEATS:
                            copy_qk(nxt, QK_BEATS.index(i))
                    if "maxima" in stages and i >= HEADS:
                        take_max(nxt, i - HEADS)
                    if "finish" in stages:
                        if i in (20, 21):
                            normalise(b, i - 20)
                        if i == 23:
                            residual1(b)
                        if i == 25:
                            norm1(b)
                        if i == 27:
                            route_logits(b)
                        if i == 29:
                            route_scores(b)
                        if i == 30:
                            copy_scoreT(b)
                        if i == 31:
                            if "maxima" in stages:
                                negate_max(nxt)
                            for k in (1, 3):
                                copy_spread(b, k)

            schedule(dve, start, frame)

        @block.gpsimd
        def _(pool):
            def add_bo(b):
                pool.wait_ge(x_loaded[b.parity], b.pair * 16 + 16)
                if not b.at_start(1):
                    pool.wait_ge(done_read, b.n * DONE - 2 * DONE + 4)
                for t in range(TILES):
                    last = pool.tensor_tensor(x_bo[:, b.parity, t, :], x_tok[:, b.parity, t, :], bo_sb[:], ALU.add)
                last.then_inc(x_bo_ready, 1)

            def rotate(b, t):
                pool.wait_ge(prep_read, b.n * PREP + 2 + t)
                if t == 0 and not b.at_start():
                    pool.wait_ge(split_ready, b.n * 2)
                table = [rope_sb[:, i, t].unsqueeze(1).to_broadcast([P, 2 * HEADS, HD]) for i in range(2)]
                pool.tensor_tensor(rope_cos[:, t], qk[:, t], table[0], ALU.mult).then_inc(rope_terms, 1)
                pairs = [a.rearrange("p h (c two) -> p h c two", two=2) for a in (rope_sin[:, t], qk[:, t], table[1])]
                for i in range(2):
                    last = pool.tensor_tensor(pairs[0][:, :, :, i], pairs[1][:, :, :, 1 - i], pairs[2][:, :, :, i],
                                              ALU.mult)
                last.then_inc(rope_terms, 1)
                pool.wait_ge(rope_terms, b.n * 2 * TILES + 2 * t + 2)
                pool.tensor_tensor(rot[:, :, t], rope_cos[:, t].rearrange("p (w h) d -> p w (h d)", w=2),
                                   rope_sin[:, t].rearrange("p (w h) d -> p w (h d)", w=2),
                                   ALU.add).then_inc(roped, 1)

            def cut_pair(b, k):
                wait_apart(pool, exp_done, b.n * HEADS + 2 * k + 2)
                block_ = probs[:, 2 * k:2 * k + 2, 0:2 * P].rearrange("p h (t q) -> p h t q", q=P)
                pool.affine_select(out=block_, in_=block_, compare_op=ALU.is_ge, fill=0.0, base=0,
                                   pattern=[[0, 2], [0, 2], [1, P]], channel_multiplier=-1).then_inc(cut, 1)

            def scale_hidden(b, e):
                if e == 0:
                    pool.wait_ge(done_read, b.n * DONE + DONE)
                if e >= 2 or not b.at_start():
                    pool.wait_ge(expert_added, b.n * EXPERTS + e - 1)
                pool.wait_ge(hid_ready, b.n * EXPERTS + e + 1)
                pool.tensor_tensor(hid_scaled[:, e % 2], hid[:, e % 2],
                                   score_all[:, b.parity, e].unsqueeze(1).to_broadcast([P, HT, SEQ]),
                                   ALU.mult).then_inc(hid_scaled_ready, 1)

            def inverse_root(b, var, rstd, step, ready):
                pool.wait_ge(step, b.n * LN + LN)
                pool.tensor_tensor(rstd[:], var[:], neg_half[:], ALU.pow).then_inc(ready, 1)

            def start():
                for t in (split, v_aug):
                    pool.memset(t[:], 0.0).then_inc(zeroed, 1)
                pool.memset(neg_half[:], -0.5).then_inc(padded, 1)
                pool.iota(iota[:], pattern=[[1, EXPERTS]], base=0, channel_multiplier=0,
                          allow_small_or_imprecise_dtypes=True).then_inc(padded, 1)
                pool.wait_ge(zeroed, 2)
                pool.memset(split[:, 1, :, :, MAX_ROW], 1.0).then_inc(padded, 1)
                for p in range(2):
                    pool.memset(v_aug[:, p, :, :, HD], 1.0).then_inc(padded, 1)
                pool.wait_ge(tables_loaded, TABLES)
                b = Batch(0, 0)
                add_bo(b)
                for t in range(TILES):
                    rotate(b, t)

            def frame(b, stages):
                nxt, prev, old = b.shift(1), b.shift(-1), b.shift(-2)
                for i in range(2 * HEADS):
                    if "prepare" in stages:
                        if i == 0:
                            add_bo(nxt)
                        if i in (3, 4):
                            rotate(nxt, i - 3)
                    if "emit" in stages and i == 2:
                        inverse_root(old, var2, rstd2, ln2_step, rstd2_ready)
                    if "attend" in stages and i < HEADS and i % 2:
                        cut_pair(b, i // 2)
                    if "experts" in stages and i - 2 in HIDDEN_BEATS:
                        scale_hidden(prev, HIDDEN_BEATS.index(i - 2))
                    if "finish" in stages and i == 24:
                        inverse_root(b, var1, rstd1, ln1_step, rstd1_ready)

            schedule(pool, start, frame)


def kernel(**inputs):
    import concourse.bacc as bacc
    from concourse.bass_utils import run_bass_kernel_spmd

    f32 = np.float32
    inv_freq = (f32(1.0) / f32(10000.0) ** (np.arange(0, HD, 2, dtype=f32) / f32(HD))).astype(f32)
    angle = np.arange(SEQ, dtype=f32)[:, None] * inv_freq[None, :]
    cos = np.repeat(np.cos(angle), 2, axis=1)
    sin = np.repeat(np.sin(angle), 2, axis=1)
    sin[:, 0::2] *= -1
    rope = np.stack([cos, sin]).reshape(2, TILES, P, HD).transpose(2, 0, 1, 3)
    mask = np.zeros((P, SEQ), f32)
    mask[:, P:] = np.where(np.arange(P)[None, :] > np.arange(P)[:, None], f32(MASKED), f32(0))
    pick = np.zeros((2, EXPERTS, EXPERTS, P), f32)
    for e in range(EXPERTS):
        pick[:, e, e, :] = 1
    tables = {"rope": rope, "mask": mask, "ident": np.eye(P, dtype=f32), "pick": pick.reshape(2 * EXPERTS, EXPERTS, P)}

    names = ["L0_attn_x", "L0_attn_wq", "L0_attn_bq", "L0_attn_wk", "L0_attn_bk", "L0_attn_wv", "L0_attn_bv",
             "L0_attn_wo", "L0_attn_bo", "L0_ffn_Wg", "L0_ffn_W1", "L0_ffn_b1", "L0_ffn_W2", "L0_ffn_b2"]
    nc = bacc.Bacc("TRN2", target_bir_lowering=False, num_devices=1)
    arrays, args = {}, []
    for name, a in [(n, inputs[n]) for n in names] + list(tables.items()):
        a = np.ascontiguousarray(a)
        arrays[f"in_{name}"] = a
        args.append(nc.dram_tensor(f"in_{name}", a.shape, mybir.dt.from_np(a.dtype), kind="ExternalInput").ap())
    out = nc.dram_tensor("out", (BATCHES, SEQ, D), F32, kind="ExternalOutput").ap()
    layer(nc, *args, out)
    r = run_bass_kernel_spmd(nc, [arrays], core_ids=[0])
    return r.results[0]["out"]
```

```python
from contextlib import ExitStack

import numpy as np

import concourse.bass as bass
from concourse import mybir

F32 = mybir.dt.float32
F32R = mybir.dt.float32r
U32 = mybir.dt.uint32
ALU = mybir.AluOpType
ACT = mybir.ActivationFunctionType

P = 128
BATCHES, SEQ, D = 16, 256, 128
HEADS = 16
HD = D // HEADS
TILES = SEQ // P
ROWS = 32
GROUP = P // ROWS
GROUPS = HEADS // GROUP
MAX_ROW = 3 * HD
EXPERTS, HIDDEN = 8, 256
HT = HIDDEN // P
UNITS = EXPERTS * HT
PAIR = 2 * SEQ
EPS = 1e-5
SCALE = float(1.0 / np.sqrt(np.float32(HD)))
MASKED = -1e9 / SCALE
CAUSAL = SEQ + P
BANK = 512

FRAME = 128
LOAD = -224
ADD_BO = 10
TURN_X = -128
COPY_XT = -122
PROJECT = (-122, -110)
BIAS_QKV = (-120, -109)
ROTATE = (-113, -108)
SPLIT_QK = -90
TURN_QK = (-81, -72, -57, -28)
COPY_QK = (-82, -72, -44, -21)
MAXIMA = (-65, -61, -56, -48, -33, -26, -20, -14, -4, 0, 11, 18, 26, 32, 41, 49)
NEGATE_MAX = (-11, 56)
TURN_QUERIES = (-3, 63)
COPY_QUERIES = (-4, 66)
SCORES = (8, 18, 24, 31, 38, 45, 58, 64, 70, 77, 87, 100, 103, 109, 115, 125)
CUT = (27, 30, 43, 54, 73, 103, 103, 119)
TIMES_V = (55, 75, 127, 130)
COPY_O = (116, 136)
TURN_O = (155, 169)
NORMALISE = (157, 171)
TURN_ATTN = 188
COPY_ATTNT = 189
PROJECT_O = 194
RESIDUAL1 = 198
ROOT1 = 186
NORM1 = 224
TURN_X1 = 230
COPY_X1T = 231
ROUTE = 237
ROUTE_LOGITS = 249
ROUTE_EXP = 244
ROUTE_SCORES = 254
TURN_SCORE = 268
COPY_SCORET = 268
SAVE_SCORE = 242
SPLIT_X1 = 385
HIDDEN_PRODUCT = (399, 405, 426, 452, 466, 479, 493, 506, 510, 525, 532, 551, 573, 581, 611, 627)
RELU = (414, 426, 453, 459, 482, 485, 497, 512, 514, 520, 539, 550, 575, 611, 631, 643)
SCALE_HIDDEN = (431, 437, 441, 443, 459, 462, 495, 507, 509, 547, 547, 560, 571, 624, 634, 645)
HIDDEN_HIGH = (443, 461, 463, 491, 494, 514, 518, 534, 541, 559, 577, 586, 620, 645, 646, 658)
HIDDEN_LOW = (441, 476, 483, 497, 504, 513, 528, 533, 542, 572, 587, 613, 625, 656, 665, 670)
LOAD_SCORES = (397, 444)
OPEN_Y = 445
ADD_UNIT = (461, 485, 488, 506, 513, 542, 548, 553, 592, 615, 625, 637, 641, 670, 675, 680)
COPY_Y = 681
TURN_Y = 687
COPY_Z2 = 692
MOMENTS2 = 692
ROOT2 = 695
NORM2 = 715
STORE = 729
SPLIT_W = (1, 19, 56, 74)
PREPARED_BEFORE = sum(beat + FRAME < TURN_QUERIES[1] for beat in (TURN_X, *PROJECT, *TURN_QK))

PREP, DONE, RT, LN1 = 7, 7, 11, 5
LN2 = 9
TABLES = 16 * 13


class Batch:

    def __init__(self, pair, parity):
        self.pair, self.parity = pair, parity

    @property
    def n(self):
        return self.pair * 2 + self.parity

    def shift(self, k):
        m = self.parity + k
        return Batch(self.pair + m // 2, m % 2)

    @property
    def peeled(self):
        return isinstance(self.pair, int)

    def at_start(self, k=0):
        return self.peeled and self.n <= k


def due(steps, beat, frame, of_pair=False):
    for k, s in enumerate(steps if isinstance(steps, tuple) else (steps,)):
        if (s - beat) % FRAME == 0:
            b = frame.shift(-((s - beat) // FRAME))
            if (not b.peeled or 0 <= b.n < BATCHES) and not (of_pair and b.parity):
                yield b, k


def layer(nc, x, wq, bq, wk, bk, wv, bv, wo, bo, wg, w1, b1, w2, b2, rope, mask, ident, score_rows, out):
    with ExitStack() as ctx:
        def sb(name, shape, dt=F32):
            return ctx.enter_context(nc.sbuf_tensor(name, shape, dt))

        def bank(name):
            return ctx.enter_context(nc.psum_tensor(name, [P, BANK], F32))

        def sem(name):
            return ctx.enter_context(nc.semaphore(name))

        wqkv = sb("wqkv", [P, 3 * D])
        bqkv = sb("bqkv", [P, 3 * D])
        wo_sb = sb("wo_sb", [P, D])
        bo_sb = sb("bo_sb", [P, D])
        wg_sb = sb("wg_sb", [P, EXPERTS])
        w1_all = sb("w1_all", [P, UNITS, P])
        w1_low = sb("w1_low", [P, UNITS, P], F32R)
        w1_high = sb("w1_high", [P, UNITS, P], F32R)
        w2_all = sb("w2_all", [P, UNITS, D])
        w2_low = sb("w2_low", [P, UNITS, D], F32R)
        w2_high = sb("w2_high", [P, UNITS, D], F32R)
        b1_rows = sb("b1_rows", [UNITS, P])
        b1_cols = sb("b1_cols", [P, UNITS])
        b2_sb = sb("b2_sb", [EXPERTS, D])
        rope_sb = sb("rope_sb", [P, 2, TILES, HD])
        mask_sb = sb("mask_sb", [P, SEQ])
        ident_sb = sb("ident_sb", [P, P])
        ident_r = sb("ident_r", [P, P], F32R)
        iota = sb("iota", [P, EXPERTS])
        spare = sb("spare", [P, 1])
        neg_half = sb("neg_half", [P, 2 * TILES])

        x_tok = sb("x_tok", [P, 2, TILES, D])
        x_bo = sb("x_bo", [P, 2, TILES, D])
        xT = sb("xT", [P, SEQ])
        qk = sb("qk", [P, TILES, 2 * HEADS, HD])
        rope_cos = sb("rope_cos", [P, TILES, 2 * HEADS, HD])
        rope_sin = sb("rope_sin", [P, TILES, 2 * HEADS, HD])
        rot = sb("rot", [P, 2, TILES, HEADS, HD])
        split = sb("split", [P, 2, 2, TILES, HEADS, ROWS])
        kT = sb("kT", [P, 2, GROUPS, SEQ], F32R)
        qT_max = sb("qT_max", [P, GROUPS, SEQ], F32R)
        qT = sb("qT", [P, GROUPS, SEQ], F32R)
        v_aug = sb("v_aug", [P, 2, TILES, HEADS, ROWS])
        junk = sb("junk", [P, 2, TILES, SEQ])
        row_max = sb("row_max", [P, TILES, HEADS])
        probs = sb("probs", [P, HEADS, CAUSAL])
        oT = sb("oT", [P, GROUPS, SEQ])
        recip = sb("recip", [P, TILES, HEADS])
        attn = sb("attn", [P, TILES, HEADS, HD])
        attnT = sb("attnT", [P, SEQ])
        z1 = sb("z1", [P, TILES, D])
        stats1 = sb("stats1", [P, TILES, 6])
        mv1 = sb("mv1", [P, TILES, 2])
        var1 = sb("var1", [P, TILES])
        rstd1 = sb("rstd1", [P, TILES])
        x1 = sb("x1", [P, TILES, D])
        x1T = sb("x1T", [P, 2, SEQ])
        x1T_high = sb("x1T_high", [P, PAIR], F32R)
        x1T_low = sb("x1T_low", [P, PAIR], F32R)
        logits = sb("logits", [P, TILES, EXPERTS])
        top_logits = sb("top_logits", [P, TILES, 8])
        neg_top = sb("neg_top", [P, TILES])
        expd = sb("expd", [P, TILES, EXPERTS])
        top = sb("top", [P, TILES, 8])
        top_at = sb("top_at", [P, TILES, 8], U32)
        top_atf = sb("top_atf", [P, TILES, 2])
        top_sum = sb("top_sum", [P, TILES])
        top_inv = sb("top_inv", [P, TILES])
        hot = sb("hot", [P, 2, TILES, EXPERTS])
        hot_sum = sb("hot_sum", [P, TILES, EXPERTS])
        score = sb("score", [P, TILES, EXPERTS])
        scoreT = sb("scoreT", [EXPERTS, 2, SEQ])
        score_all = sb("score_all", [P, EXPERTS, PAIR])
        hid = sb("hid", [P, 2, PAIR])
        hid_scaled = sb("hid_scaled", [P, 4, PAIR])
        hid_low = sb("hid_low", [P, 4, PAIR], F32R)
        hid_high = sb("hid_high", [P, 4, PAIR], F32R)
        yT = sb("yT", [P, PAIR])
        z2 = sb("z2", [P, 2 * TILES, D])
        stats2 = sb("stats2", [P, 2 * TILES, 6])
        mv2 = sb("mv2", [P, 2 * TILES, 2])
        var2 = sb("var2", [P, 2 * TILES])
        rstd2 = sb("rstd2", [P, 2 * TILES])
        out_tok = sb("out_tok", [P, 2 * TILES, D])

        ps_score = bank("ps_score")
        ps_max = bank("ps_max")
        ps_pv = bank("ps_pv")
        ps_hid = [bank("ps_hid0"), bank("ps_hid1")]
        ps_y = bank("ps_y")
        ps_prep = bank("ps_prep")
        ps_done = bank("ps_done")

        tables_loaded = sem("tables_loaded")
        w_loaded = sem("w_loaded")
        zeroed = sem("zeroed")
        padded = sem("padded")
        b1_turned = sem("b1_turned")
        setup_done = sem("setup_done")
        w_high = sem("w_high")
        w_split = sem("w_split")
        x_loaded = [sem("x_loaded0"), sem("x_loaded1")]
        x_bo_ready = sem("x_bo_ready")
        prep_full = sem("prep_full")
        prep_read = sem("prep_read")
        rope_terms = sem("rope_terms")
        roped = sem("roped")
        high_ready = sem("high_ready")
        split_ready = sem("split_ready")
        max_full = sem("max_full")
        max_read = sem("max_read")
        neg_max_ready = sem("neg_max_ready")
        qT_full = sem("qT_full")
        qT_read = sem("qT_read")
        scores_full = sem("scores_full")
        exp_done = sem("exp_done")
        cut = sem("cut")
        pv_full = sem("pv_full")
        pv_read = sem("pv_read")
        done_full = sem("done_full")
        done_read = sem("done_read")
        recip_ready = sem("recip_ready")
        ln1_step = sem("ln1_step")
        rstd1_ready = sem("rstd1_ready")
        x1_ready = sem("x1_ready")
        route_step = sem("route_step")
        scored = sem("scored")
        route_exp = sem("route_exp")
        score_saved = [sem("score_saved0"), sem("score_saved1")]
        score_loaded = [sem("score_loaded0"), sem("score_loaded1")]
        x1_high_ready = sem("x1_high_ready")
        x1_split = sem("x1_split")
        hid_full = sem("hid_full")
        hid_ready = sem("hid_ready")
        hid_scaled_ready = sem("hid_scaled_ready")
        hid_high_ready = sem("hid_high_ready")
        hid_split = sem("hid_split")
        unit_added = sem("unit_added")
        y_read = sem("y_read")
        emit_full = sem("emit_full")
        emit_read = sem("emit_read")
        ln2_step = sem("ln2_step")
        rstd2_ready = sem("rstd2_ready")
        out_ready = sem("out_ready")
        stored = sem("stored")

        def schedule(eng, at_beat):
            def frame(b):
                for beat in range(FRAME):
                    at_beat(b, beat)

            for n in range(-1, 4):
                frame(Batch(n // 2, n % 2))
            with eng.Fori(2, BATCHES // 2 - 1) as pair:
                for parity in range(2):
                    frame(Batch(pair, parity))
            for n in range(BATCHES - 2, BATCHES + 4):
                frame(Batch(n // 2, n % 2))

        def value(eng, count):
            return count if isinstance(count, int) else eng.to_reg(count)

        def wait_apart(eng, semaphore, count):
            count = value(eng, count)
            eng.wait_ge(tables_loaded, TABLES)
            eng.wait_ge(semaphore, count)

        block = ctx.enter_context(nc.Block())

        @block.sync
        def _(sp):
            def load(b):
                src = x[bass.ds(b.n, 1)].rearrange("a (t p) d -> p (a t) d", p=P)
                sp.dma_start(x_tok[:, b.parity], src).then_inc(x_loaded[b.parity], 16)

            def save_score(b):
                sp.wait_ge(done_read, b.n * DONE + DONE)
                sp.dma_start(score_rows[:, bass.ds(b.n, 1), :], scoreT[:, b.parity:b.parity + 1, :]
                             ).then_inc(score_saved[b.parity], 16)

            def load_scores(b, half):
                n = EXPERTS // 2
                saved, used = value(sp, b.pair * 16 + 16), value(sp, b.pair * UNITS + (half - 1) * UNITS // 2)
                if half == 0:
                    for s in score_saved:
                        sp.wait_ge(s, saved)
                if not b.at_start():
                    sp.wait_ge(hid_scaled_ready, used)
                src = score_rows[half * n:(half + 1) * n, bass.ds(b.n, 2), :].rearrange("e b s -> e (b s)")
                sp.dma_start(score_all[:, half * n:(half + 1) * n, :], src.partition_broadcast(P)
                             ).then_inc(score_loaded[half], 16)

            def store(b):
                sp.wait_ge(out_ready, b.pair * 2 * TILES + 2 * TILES)
                dst = out[bass.ds(b.n, 2)].rearrange("a (t p) d -> p (a t) d", p=P)
                sp.dma_start(dst, out_tok[:]).then_inc(stored, 16)

            load(Batch(0, 0))
            for i, (w, b) in enumerate(((wq, bq), (wk, bk), (wv, bv))):
                sp.dma_start(wqkv[:, i * D:(i + 1) * D], w).then_inc(tables_loaded, 16)
                sp.dma_start(bqkv[:, i * D:(i + 1) * D], b.partition_broadcast(P)).then_inc(tables_loaded, 16)
            sp.dma_start(ident_sb[:], ident).then_inc(tables_loaded, 16)
            sp.dma_start(rope_sb[:], rope).then_inc(tables_loaded, 16)
            sp.dma_start(mask_sb[:], mask).then_inc(tables_loaded, 16)
            sp.dma_start(bo_sb[:], bo.partition_broadcast(P)).then_inc(tables_loaded, 16)
            sp.dma_start(wo_sb[:], wo).then_inc(tables_loaded, 16)
            sp.dma_start(wg_sb[:], wg).then_inc(tables_loaded, 16)
            sp.dma_start(b1_rows[:], b1.rearrange("e (t p) -> (e t) p", p=P)).then_inc(tables_loaded, 16)
            load(Batch(0, 1))
            sp.dma_start(w1_all[:].rearrange("p (e t) q -> p e (t q)", t=HT), w1.rearrange("e d h -> d e h")).then_inc(w_loaded, 16)
            sp.dma_start(w2_all[:], w2.rearrange("e (t p) d -> p (e t) d", p=P)).then_inc(w_loaded, 16)
            sp.dma_start(b2_sb[:], b2).then_inc(w_loaded, 16)

            def at_beat(frame, beat):
                for b, _ in due(LOAD, beat, frame):
                    if not b.at_start(1):
                        turned, added = value(sp, (b.n - 2) * PREP + 1), value(sp, b.n - 1)
                        sp.wait_ge(prep_full, turned)
                        sp.wait_ge(x_bo_ready, added)
                        load(b)
                for b, _ in due(SAVE_SCORE, beat, frame):
                    save_score(b)
                for b, half in due(LOAD_SCORES, beat, frame, of_pair=True):
                    load_scores(b, half)
                for b, _ in due(STORE, beat, frame, of_pair=True):
                    store(b)

            schedule(sp, at_beat)
            sp.wait_ge(stored, 16 + 16 * BATCHES // 2)

        @block.tensor
        def _(pe):
            def turn(dst, src, n=P):
                return pe.transpose(dst, src, ident_sb[:n, :n])

            def prep_fill(b, k):
                if k:
                    pe.wait_ge(prep_read, b.n * PREP + k)
                if not b.at_start():
                    if k == PREPARED_BEFORE:
                        pe.wait_ge(qT_read, b.n * 2)
                    elif k == 0:
                        pe.wait_ge(qT_read, b.n * 2 - 1)

            def turn_x(b):
                prep_fill(b, 0)
                pe.wait_ge(x_loaded[b.parity], b.pair * 16 + 16)
                for t in range(TILES):
                    last = turn(ps_prep[:, t * P:(t + 1) * P], x_tok[:, b.parity, t, :])
                last.then_inc(prep_full, 1)

            def project(b, t):
                prep_fill(b, 1 + t)
                pe.matmul(ps_prep[:, 0:3 * D], xT[:, t * P:(t + 1) * P], wqkv[:], start=True,
                          stop=True).then_inc(prep_full, 1)

            def turn_split(b, which, half):
                for g in range(2):
                    for t in range(TILES):
                        src = split[:, b.parity, which, t, (2 * half + g) * GROUP:(2 * half + g + 1) * GROUP, :]
                        last = turn(ps_prep[:, g * SEQ + t * P:g * SEQ + (t + 1) * P],
                                    src.rearrange("p h r -> p (h r)"))
                return last

            def turn_qk(b, i):
                prep_fill(b, 3 + i)
                if i == 0:
                    pe.wait_ge(split_ready, b.n * 2 + 2)
                turn_split(b, 1 - i % 2, i // 2).then_inc(prep_full, 1)

            def turn_queries(b, half):
                pe.wait_ge(neg_max_ready, b.n * 2 + half + 1)
                if half == 0:
                    pe.wait_ge(prep_read, b.n * PREP + PREP)
                    if PREPARED_BEFORE == PREP and not b.at_start():
                        pe.wait_ge(qT_read, b.n * 2)
                else:
                    last = b.peeled and b.n == BATCHES - 1
                    pe.wait_ge(prep_read, b.n * PREP + PREP + (0 if last else PREPARED_BEFORE))
                    if PREPARED_BEFORE == 0 or last:
                        pe.wait_ge(qT_read, b.n * 2 + 1)
                turn_split(b, 0, half).then_inc(qT_full, 1)

            def max_scores(b, h):
                g, r = h // GROUP, h % GROUP * ROWS
                if h or not b.at_start():
                    pe.wait_ge(max_read, b.n * HEADS + h)
                if h % (HEADS // 2) == 0:
                    pe.wait_ge(prep_read, b.n * PREP + 5 + h // (HEADS // 2) * 2)
                for t in range(TILES):
                    last = pe.matmul(ps_max[:, t * SEQ:(t + 1) * SEQ],
                                     qT_max[r:r + MAX_ROW, g, t * P:(t + 1) * P],
                                     kT[r:r + MAX_ROW, b.parity, g, :], start=True, stop=True)
                last.then_inc(max_full, 1)

            def scores(b, h):
                g, r = h // GROUP, h % GROUP * ROWS
                if h % (HEADS // 2) == 0:
                    pe.wait_ge(qT_read, b.n * 2 + 1 + h // (HEADS // 2))
                if h or not b.at_start():
                    pe.wait_ge(exp_done, b.n * HEADS + h)
                for i, t in enumerate(reversed(range(TILES))):
                    last = pe.matmul(ps_score[:, i * SEQ:(i + 1) * SEQ],
                                     kT[r:r + ROWS, b.parity, g, t * P:(t + 1) * P],
                                     qT[r:r + ROWS, g, :], start=True, stop=True)
                last.then_inc(scores_full, 1)

            def times_v(b, g):
                pe.wait_ge(cut, b.n * (HEADS // 2) + 2 * g + 2)
                if g == 2:
                    pe.wait_ge(pv_read, b.n * 2 + 1)
                elif g == 0 and not b.at_start():
                    pe.wait_ge(pv_read, b.n * 2)
                for j in range(GROUP):
                    h, c = g * GROUP + j, g % 2 * SEQ
                    dst = ps_pv[j * ROWS:(j + 1) * ROWS, :]
                    pe.matmul(dst[:, c:c + SEQ], v_aug[:, b.parity, 0, h, :], probs[:, h, P:CAUSAL],
                              start=True, stop=False)
                    last = pe.matmul(dst[:, c + P:c + SEQ], v_aug[:, b.parity, 1, h, :], probs[:, h, 0:P],
                                     start=False, stop=True)
                if g % 2:
                    last.then_inc(pv_full, 1)

            def done_fill(b, k):
                if k:
                    pe.wait_ge(done_read, b.n * DONE + k)
                elif not b.at_start():
                    pe.wait_ge(done_read, b.n * DONE)

            def turn_o(b, t):
                done_fill(b, t)
                if t == 0:
                    pe.wait_ge(pv_read, b.n * 2 + 2)
                for g in range(GROUPS):
                    last = turn(ps_done[:, g * P:(g + 1) * P], oT[:, g, t * P:(t + 1) * P])
                last.then_inc(done_full, 1)

            def turn_attn(b):
                done_fill(b, 2)
                for t in range(TILES):
                    last = turn(ps_done[:, t * P:(t + 1) * P], attn[:, t].rearrange("p h d -> p (h d)"))
                last.then_inc(done_full, 1)

            def project_o(b):
                done_fill(b, 3)
                for t in range(TILES):
                    last = pe.matmul(ps_done[:, t * P:(t + 1) * P], attnT[:, t * P:(t + 1) * P], wo_sb[:],
                                     start=True, stop=True)
                last.then_inc(done_full, 1)

            def turn_x1(b):
                done_fill(b, 4)
                pe.wait_ge(x1_ready, b.n * TILES + TILES)
                for t in range(TILES):
                    last = turn(ps_done[:, t * P:(t + 1) * P], x1[:, t, :])
                last.then_inc(done_full, 1)

            def route(b):
                done_fill(b, 5)
                for t in range(TILES):
                    last = pe.matmul(ps_done[:, t * EXPERTS:(t + 1) * EXPERTS],
                                     x1T[:, b.parity, t * P:(t + 1) * P], wg_sb[:], start=True, stop=True)
                last.then_inc(done_full, 1)

            def turn_score(b):
                done_fill(b, 6)
                pe.wait_ge(scored, b.n * 2 + 2)
                for t in range(TILES):
                    last = turn(ps_done[0:EXPERTS, t * P:(t + 1) * P], score[:, t, :])
                last.then_inc(done_full, 1)

            def products(dst, w_high, w_low, rows_high, rows_low, start, stop):
                pe.matmul(dst, w_high, rows_high, start=start, stop=False)
                pe.matmul(dst, w_low, rows_high, start=False, stop=False)
                return pe.matmul(dst, w_high, rows_low, start=False, stop=stop)

            def hidden(b, i):
                if i == 0:
                    pe.wait_ge(x1_split, b.pair + 1)
                    if b.at_start():
                        pe.wait_ge(w_split, len(SPLIT_W))
                if i >= 2 or not b.at_start():
                    pe.wait_ge(hid_ready, b.pair * UNITS + i - 1)
                products(ps_hid[i % 2][:], w1_high[:, i, :], w1_low[:, i, :], x1T_high[:], x1T_low[:],
                         True, True).then_inc(hid_full, 1)

            def open_y(b):
                pe.wait_ge(done_read, b.n * DONE + 2 * DONE)
                if not b.at_start():
                    pe.wait_ge(emit_read, b.pair)
                pe.matmul(ps_y[:], b2_sb[:], scoreT[:].rearrange("e b s -> e (b s)"), start=True, stop=False)
                for part in (x1T_high, x1T_low):
                    pe.matmul(ps_y[:], ident_r[:], part[:], start=False, stop=False)

            def add_unit(b, i):
                pe.wait_ge(hid_split, b.pair * UNITS + i + 1)
                products(ps_y[:], w2_high[:, i, :], w2_low[:, i, :], hid_high[:, i % 4, :],
                         hid_low[:, i % 4, :], False, i == UNITS - 1).then_inc(unit_added, 1)

            def turn_y(b):
                pe.wait_ge(y_read, b.pair + 1)
                for t in range(2 * TILES):
                    last = turn(ps_y[:, t * P:(t + 1) * P], yT[:, t * P:(t + 1) * P])
                last.then_inc(emit_full, 1)

            pe.wait_ge(tables_loaded, TABLES)
            turn(ps_done[:, 0:UNITS], b1_rows[:], UNITS).then_inc(b1_turned, 1)
            pe.wait_ge(setup_done, 2)

            def at_beat(frame, beat):
                for b, h in due(SCORES, beat, frame):
                    scores(b, h)
                for b, h in due(MAXIMA, beat, frame):
                    max_scores(b, h)
                for b, half in due(TURN_QUERIES, beat, frame):
                    turn_queries(b, half)
                for b, _ in due(TURN_X, beat, frame):
                    turn_x(b)
                for b, t in due(PROJECT, beat, frame):
                    project(b, t)
                for b, i in due(TURN_QK, beat, frame):
                    turn_qk(b, i)
                for b, g in due(TIMES_V, beat, frame):
                    times_v(b, g)
                for b, i in due(HIDDEN_PRODUCT, beat, frame, of_pair=True):
                    hidden(b, i)
                for b, t in due(TURN_O, beat, frame):
                    turn_o(b, t)
                for b, _ in due(TURN_ATTN, beat, frame):
                    turn_attn(b)
                for b, _ in due(PROJECT_O, beat, frame):
                    project_o(b)
                for b, _ in due(TURN_X1, beat, frame):
                    turn_x1(b)
                for b, _ in due(ROUTE, beat, frame):
                    route(b)
                for b, _ in due(TURN_SCORE, beat, frame):
                    turn_score(b)
                for b, _ in due(TURN_Y, beat, frame, of_pair=True):
                    turn_y(b)
                for b, _ in due(OPEN_Y, beat, frame, of_pair=True):
                    open_y(b)
                for b, i in due(ADD_UNIT, beat, frame, of_pair=True):
                    add_unit(b, i)

            schedule(pe, at_beat)

        @block.scalar
        def _(act):
            def copy_xT(b):
                act.wait_ge(prep_full, b.n * PREP + 1)
                act.activation(xT[:], ps_prep[:, 0:SEQ], ACT.Copy).then_inc(prep_read, 1)

            def exponent(b, h):
                act.wait_ge(scores_full, b.n * HEADS + h + 1)
                act.activation(probs[:, h, :], ps_score[:, P:P + CAUSAL], ACT.Exp,
                               scale=SCALE).then_inc(exp_done, 1)

            def copy_o(b, half):
                act.wait_ge(pv_full, b.n * 2 + half + 1)
                act.activation(oT[:, 2 * half:2 * half + 2, :].rearrange("p g s -> p (g s)"), ps_pv[:],
                               ACT.Copy).then_inc(pv_read, 1)

            def copy_done(b, k, dst, n):
                act.wait_ge(done_full, b.n * DONE + k + 1)
                act.activation(dst, ps_done[:, 0:n], ACT.Copy).then_inc(done_read, 1)

            def route_exponent(b):
                act.wait_ge(route_step, b.n * RT + 3)
                for t in range(TILES):
                    act.activation(expd[:, t, :], logits[:, t, :], ACT.Exp,
                                   bias=neg_top[:, t:t + 1]).then_inc(route_exp, 1)

            def split_w(k):
                act.wait_ge(w_loaded, 48)
                part = slice(k * UNITS // len(SPLIT_W), (k + 1) * UNITS // len(SPLIT_W))
                act.activation(w1_high[:, part, :], w1_all[:, part, :], ACT.Copy)
                act.activation(w2_high[:, part, :], w2_all[:, part, :], ACT.Copy).then_inc(w_high, 1)

            def split_x1(b):
                if not b.at_start():
                    act.wait_ge(hid_full, b.pair * UNITS)
                act.wait_ge(done_read, b.n * DONE + DONE + 5)
                act.activation(x1T_high[:], x1T[:].rearrange("p b s -> p (b s)"), ACT.Copy
                               ).then_inc(x1_high_ready, 1)

            def relu(b, i):
                if i >= 2 or not b.at_start():
                    act.wait_ge(hid_scaled_ready, b.pair * UNITS + i - 1)
                act.wait_ge(hid_full, b.pair * UNITS + i + 1)
                act.activation(hid[:, i % 2, :], ps_hid[i % 2][:], ACT.Relu,
                               bias=b1_cols[:, i:i + 1]).then_inc(hid_ready, 1)

            def hidden_high(b, i):
                act.wait_ge(hid_scaled_ready, b.pair * UNITS + i + 1)
                act.activation(hid_high[:, i % 4, :], hid_scaled[:, i % 4, :], ACT.Copy
                               ).then_inc(hid_high_ready, 1)

            def copy_y(b):
                act.wait_ge(unit_added, b.pair * UNITS + UNITS)
                act.activation(yT[:], ps_y[:], ACT.Copy).then_inc(y_read, 1)

            def copy_z2(b):
                act.wait_ge(emit_full, b.pair + 1)
                if not b.at_start():
                    act.wait_ge(out_ready, b.pair * 2 * TILES)
                act.activation(z2[:].rearrange("p t d -> p (t d)"), ps_y[:], ACT.Copy
                               ).then_inc(emit_read, 1)

            act.wait_ge(setup_done, 2)

            def at_beat(frame, beat):
                for b, h in due(SCORES, beat, frame):
                    exponent(b, h)
                for b, _ in due(COPY_XT, beat, frame):
                    copy_xT(b)
                for b, half in due(COPY_O, beat, frame):
                    copy_o(b, half)
                for b, _ in due(COPY_ATTNT, beat, frame):
                    copy_done(b, 2, attnT[:], SEQ)
                for b, _ in due(COPY_X1T, beat, frame):
                    copy_done(b, 4, x1T[:, b.parity, :], SEQ)
                for b, _ in due(ROUTE_EXP, beat, frame):
                    route_exponent(b)
                for b, _ in due(SPLIT_X1, beat, frame, of_pair=True):
                    split_x1(b)
                for b, i in due(HIDDEN_HIGH, beat, frame, of_pair=True):
                    hidden_high(b, i)
                for b, i in due(RELU, beat, frame, of_pair=True):
                    relu(b, i)
                for b, _ in due(COPY_Y, beat, frame, of_pair=True):
                    copy_y(b)
                for b, _ in due(COPY_Z2, beat, frame, of_pair=True):
                    copy_z2(b)
                for b, k in due(SPLIT_W, beat, frame):
                    if b.peeled and b.n == 1:
                        split_w(k)

            schedule(act, at_beat)

        @block.vector
        def _(dve):
            def bias_qkv(b, t):
                dve.wait_ge(prep_full, b.n * PREP + 2 + t)
                if not b.at_start():
                    dve.wait_ge(roped, b.n * TILES)
                if not b.at_start(1):
                    dve.wait_ge(pv_full, b.n * 2 - 2)
                dve.tensor_tensor(qk[:, t].rearrange("p h d -> p (h d)"), ps_prep[:, 0:2 * D],
                                  bqkv[:, 0:2 * D], ALU.add)
                dve.tensor_tensor(v_aug[:, b.parity, t, :, 0:HD],
                                  ps_prep[:, 2 * D:3 * D].rearrange("p (h d) -> p h d", d=HD),
                                  bqkv[:, 2 * D:3 * D].rearrange("p (h d) -> p h d", d=HD),
                                  ALU.add).then_inc(prep_read, 1)

            def slots(b, which, first, step, n):
                rows = split[:, b.parity, which].rearrange("p t h (s d) -> p (t h) s d", d=HD)
                return rows[:, :, first:first + step * (n - 1) + 1:step, :].bitcast(F32R)

            def split_qk(b):
                dve.wait_ge(roped, b.n * TILES + TILES)
                if not b.at_start(1):
                    dve.wait_ge(qT_full, b.n * 2 - 2)
                src = [rot[:, w].rearrange("p t h d -> p (t h) d") for w in range(2)]
                for w, step in ((0, 1), (1, 2)):
                    dve.tensor_copy(slots(b, w, 0, step, 2),
                                    src[w].unsqueeze(2).to_broadcast([P, TILES * HEADS, 2, HD])
                                    ).then_inc(high_ready, 1)
                for w, low in ((0, 2), (1, 1)):
                    dve.wait_ge(high_ready, b.n * 2 + w + 1)
                    dve.tensor_tensor(slots(b, w, low, 1, 1)[:, :, 0, :], src[w],
                                      slots(b, w, 0, 1, 1)[:, :, 0, :].bitcast(F32),
                                      ALU.subtract).then_inc(split_ready, 1)

            def copy_qk(b, i):
                dve.wait_ge(prep_full, b.n * PREP + 4 + i)
                half = 2 * (i // 2)
                dst = (qT_max if i % 2 else kT[:, b.parity])[:, half:half + 2, :]
                dve.tensor_copy(dst.rearrange("p g s -> p (g s)"), ps_prep[:]).then_inc(prep_read, 1)

            def copy_queries(b, half):
                dve.wait_ge(qT_full, b.n * 2 + half + 1)
                dve.tensor_copy(qT[:, 2 * half:2 * half + 2, :].rearrange("p g s -> p (g s)"),
                                ps_prep[:]).then_inc(qT_read, 1)

            def take_max(b, h):
                wait_apart(dve, max_full, b.n * HEADS + h + 1)
                for t in range(TILES):
                    n = (t + 1) * P
                    last = dve.tensor_tensor_reduce(
                        out=junk[:, h % 2, t, 0:n], in0=ps_max[:, t * SEQ:t * SEQ + n],
                        in1=mask_sb[:, SEQ - n:SEQ], scale=1.0, scalar=-3.0e38, op0=ALU.add, op1=ALU.max,
                        accum_out=row_max[:, t, h:h + 1])
                last.then_inc(max_read, 1)

            def negate_max(b, half):
                n = HEADS // 2
                dve.wait_ge(max_read, b.n * HEADS + (half + 1) * n)
                dve.tensor_scalar(split[:, b.parity, 0, :, half * n:(half + 1) * n, MAX_ROW].bitcast(F32R),
                                  row_max[:, :, half * n:(half + 1) * n], -1.0, None,
                                  ALU.mult).then_inc(neg_max_ready, 1)

            def normalise(b, t):
                dve.wait_ge(done_full, b.n * DONE + t + 1)
                o = ps_done[:].rearrange("p (h r) -> p h r", r=ROWS)
                dve.reciprocal(recip[:, t, :], o[:, :, HD]).then_inc(recip_ready, 1)
                dve.wait_ge(recip_ready, b.n * TILES + t + 1)
                dve.tensor_tensor(attn[:, t], o[:, :, 0:HD],
                                  recip[:, t, :].unsqueeze(2).to_broadcast([P, HEADS, HD]),
                                  ALU.mult).then_inc(done_read, 1)

            def moments(n, tiles, z, stats, mv, var, step):
                for t in range(tiles):
                    dve.bn_stats(stats[:, t, :], z[:, t, :]).then_inc(step, 1)
                for t in range(tiles):
                    wait_apart(dve, step, n + t + 1)
                    dve.bn_aggr(mv[:, t, :], stats[:, t, :]).then_inc(step, 1)
                dve.wait_ge(step, n + 2 * tiles)
                dve.tensor_scalar(var[:], mv[:, :, 1], EPS, None, ALU.add).then_inc(step, 1)

            def residual1(b):
                dve.wait_ge(x_bo_ready, b.n + 1)
                dve.wait_ge(done_full, b.n * DONE + 4)
                dve.tensor_tensor(z1[:].rearrange("p t d -> p (t d)"), ps_done[:, 0:SEQ],
                                  x_bo[:, b.parity].rearrange("p t d -> p (t d)"), ALU.add).then_inc(done_read, 1)
                dve.wait_ge(done_read, b.n * DONE + 4)
                moments(b.n * LN1, TILES, z1, stats1, mv1, var1, ln1_step)

            def norm1(b):
                dve.wait_ge(rstd1_ready, b.n + 1)
                for t in range(TILES):
                    dve.tensor_scalar(x1[:, t, :], z1[:, t, :], mv1[:, t, 0:1], rstd1[:, t:t + 1],
                                      ALU.subtract, ALU.mult).then_inc(x1_ready, 1)

            def route_logits(b):
                dve.wait_ge(done_full, b.n * DONE + 6)
                dve.tensor_copy(logits[:].rearrange("p t e -> p (t e)"),
                                ps_done[:, 0:TILES * EXPERTS]).then_inc(done_read, 1)
                wait_apart(dve, done_read, b.n * DONE + 6)
                for t in range(TILES):
                    dve.max(top_logits[:, t, :], logits[:, t, :]).then_inc(route_step, 1)
                dve.wait_ge(route_step, b.n * RT + 2)
                dve.tensor_scalar(neg_top[:], top_logits[:, :, 0], -1.0, None, ALU.mult).then_inc(route_step, 1)

            def route_scores(b):
                def after(k):
                    dve.wait_ge(route_step, b.n * RT + k)

                wait_apart(dve, route_exp, b.n * TILES + TILES)
                for t in range(TILES):
                    dve.max(top[:, t, :], expd[:, t, :]).then_inc(route_step, 1)
                wait_apart(dve, route_step, b.n * RT + 5)
                for t in range(TILES):
                    dve.max_index(top_at[:, t, :], top[:, t, :], expd[:, t, :]).then_inc(route_step, 1)
                dve.tensor_tensor(top_sum[:], top[:, :, 0], top[:, :, 1], ALU.add).then_inc(route_step, 1)
                after(7)
                dve.tensor_copy(top_atf[:], top_at[:, :, 0:2]).then_inc(route_step, 1)
                after(8)
                dve.reciprocal(top_inv[:], top_sum[:]).then_inc(route_step, 1)
                after(9)
                for t in range(TILES):
                    for k in range(2):
                        last = dve.tensor_scalar(hot[:, k, t, :], iota[:], top_atf[:, t, k:k + 1],
                                                 top[:, t, k:k + 1], ALU.is_equal, ALU.mult)
                last.then_inc(route_step, 1)
                after(11)
                dve.tensor_tensor(hot_sum[:], hot[:, 0], hot[:, 1], ALU.add).then_inc(scored, 1)
                dve.wait_ge(scored, b.n * 2 + 1)
                dve.tensor_tensor(score[:], hot_sum[:], top_inv[:].unsqueeze(2).to_broadcast([P, TILES, EXPERTS]),
                                  ALU.mult).then_inc(scored, 1)

            def copy_scoreT(b):
                if not b.at_start(1):
                    dve.wait_ge(score_saved[b.parity], b.pair * 16)
                dve.wait_ge(done_full, b.n * DONE + 7)
                dve.tensor_copy(scoreT[:, b.parity, :], ps_done[0:EXPERTS, 0:SEQ]).then_inc(done_read, 1)

            def split_w(k):
                dve.wait_ge(w_high, k + 1)
                part = slice(k * UNITS // len(SPLIT_W), (k + 1) * UNITS // len(SPLIT_W))
                for low, every, high in ((w1_low, w1_all, w1_high), (w2_low, w2_all, w2_high)):
                    last = dve.tensor_tensor(low[:, part, :], every[:, part, :],
                                             high[:, part, :].bitcast(F32), ALU.subtract)
                last.then_inc(w_split, 1)

            def split_x1(b):
                dve.wait_ge(x1_high_ready, b.pair + 1)
                dve.tensor_tensor(x1T_low[:], x1T[:].rearrange("p b s -> p (b s)"), x1T_high[:].bitcast(F32),
                                  ALU.subtract).then_inc(x1_split, 1)

            def hidden_low(b, i):
                dve.wait_ge(hid_high_ready, b.pair * UNITS + i + 1)
                dve.tensor_tensor(hid_low[:, i % 4, :], hid_scaled[:, i % 4, :],
                                  hid_high[:, i % 4, :].bitcast(F32), ALU.subtract).then_inc(hid_split, 1)

            def moments2(b):
                dve.wait_ge(emit_read, b.pair + 1)
                moments(b.pair * LN2, 2 * TILES, z2, stats2, mv2, var2, ln2_step)

            def norm2(b):
                dve.wait_ge(stored, b.pair * 16 + 16)
                dve.wait_ge(rstd2_ready, b.pair + 1)
                for t in range(2 * TILES):
                    dve.tensor_scalar(out_tok[:, t, :], z2[:, t, :], mv2[:, t, 0:1], rstd2[:, t:t + 1],
                                      ALU.subtract, ALU.mult).then_inc(out_ready, 1)

            dve.wait_ge(b1_turned, 1)
            dve.tensor_copy(b1_cols[:], ps_done[:, 0:UNITS]).then_inc(setup_done, 1)
            dve.wait_ge(tables_loaded, TABLES)
            dve.tensor_copy(ident_r[:], ident_sb[:]).then_inc(setup_done, 1)
            dve.wait_ge(padded, 5)

            def at_beat(frame, beat):
                for b, half in due(NEGATE_MAX, beat, frame):
                    negate_max(b, half)
                for b, h in due(MAXIMA, beat, frame):
                    take_max(b, h)
                for b, half in due(COPY_QUERIES, beat, frame):
                    copy_queries(b, half)
                for b, t in due(BIAS_QKV, beat, frame):
                    bias_qkv(b, t)
                for b, _ in due(SPLIT_QK, beat, frame):
                    split_qk(b)
                for b, i in due(COPY_QK, beat, frame):
                    copy_qk(b, i)
                for b, t in due(NORMALISE, beat, frame):
                    normalise(b, t)
                for b, _ in due(RESIDUAL1, beat, frame):
                    residual1(b)
                for b, _ in due(NORM1, beat, frame):
                    norm1(b)
                for b, _ in due(ROUTE_LOGITS, beat, frame):
                    route_logits(b)
                for b, _ in due(ROUTE_SCORES, beat, frame):
                    route_scores(b)
                for b, _ in due(COPY_SCORET, beat, frame):
                    copy_scoreT(b)
                for b, _ in due(SPLIT_X1, beat, frame, of_pair=True):
                    split_x1(b)
                for b, i in due(HIDDEN_LOW, beat, frame, of_pair=True):
                    hidden_low(b, i)
                for b, _ in due(MOMENTS2, beat, frame, of_pair=True):
                    moments2(b)
                for b, _ in due(NORM2, beat, frame, of_pair=True):
                    norm2(b)
                for b, k in due(SPLIT_W, beat, frame):
                    if b.peeled and b.n == 1:
                        split_w(k)

            schedule(dve, at_beat)

        @block.gpsimd
        def _(pool):
            def add_bo(b):
                pool.wait_ge(x_loaded[b.parity], b.pair * 16 + 16)
                if not b.at_start(1):
                    pool.wait_ge(done_read, b.n * DONE - 2 * DONE + 4)
                for t in range(TILES):
                    last = pool.tensor_tensor(x_bo[:, b.parity, t, :], x_tok[:, b.parity, t, :], bo_sb[:], ALU.add)
                last.then_inc(x_bo_ready, 1)

            def rotate(b, t):
                pool.wait_ge(prep_read, b.n * PREP + 2 + t)
                if t == 0 and not b.at_start():
                    pool.wait_ge(split_ready, b.n * 2)
                table = [rope_sb[:, i, t].unsqueeze(1).to_broadcast([P, 2 * HEADS, HD]) for i in range(2)]
                pool.tensor_tensor(rope_cos[:, t], qk[:, t], table[0], ALU.mult).then_inc(rope_terms, 1)
                pairs = [a.rearrange("p h (c two) -> p h c two", two=2) for a in (rope_sin[:, t], qk[:, t], table[1])]
                for i in range(2):
                    last = pool.tensor_tensor(pairs[0][:, :, :, i], pairs[1][:, :, :, 1 - i], pairs[2][:, :, :, i],
                                              ALU.mult)
                last.then_inc(rope_terms, 1)
                pool.wait_ge(rope_terms, b.n * 2 * TILES + 2 * t + 2)
                pool.tensor_tensor(rot[:, :, t], rope_cos[:, t].rearrange("p (w h) d -> p w (h d)", w=2),
                                   rope_sin[:, t].rearrange("p (w h) d -> p w (h d)", w=2),
                                   ALU.add).then_inc(roped, 1)

            def cut_pair(b, k):
                wait_apart(pool, exp_done, b.n * HEADS + 2 * k + 2)
                block_ = probs[:, 2 * k:2 * k + 2, 0:2 * P].rearrange("p h (t q) -> p h t q", q=P)
                pool.affine_select(out=block_, in_=block_, compare_op=ALU.is_ge, fill=0.0, base=0,
                                   pattern=[[0, 2], [0, 2], [1, P]], channel_multiplier=-1).then_inc(cut, 1)

            def scale_hidden(b, i):
                if i % (UNITS // 2) == 0:
                    pool.wait_ge(score_loaded[i // (UNITS // 2)], b.pair * 16 + 16)
                if i >= 4 or not b.at_start():
                    pool.wait_ge(unit_added, b.pair * UNITS + i - 3)
                pool.wait_ge(hid_ready, b.pair * UNITS + i + 1)
                pool.tensor_tensor(hid_scaled[:, i % 4, :], hid[:, i % 2, :], score_all[:, i // HT, :],
                                   ALU.mult).then_inc(hid_scaled_ready, 1)

            def inverse_root(variance_ready, rstd_ready, var, rstd):
                semaphore, count = variance_ready
                pool.wait_ge(semaphore, count)
                pool.tensor_tensor(rstd[:], var[:], neg_half[:, 0:rstd.shape[1]], ALU.pow).then_inc(rstd_ready, 1)

            for t in (split, v_aug):
                pool.memset(t[:], 0.0).then_inc(zeroed, 1)
            pool.memset(neg_half[:], -0.5).then_inc(padded, 1)
            pool.iota(iota[:], pattern=[[1, EXPERTS]], base=0, channel_multiplier=0,
                      allow_small_or_imprecise_dtypes=True).then_inc(padded, 1)
            pool.wait_ge(zeroed, 2)
            pool.memset(split[:, :, 1, :, :, MAX_ROW], 1.0).then_inc(padded, 1)
            for p in range(2):
                pool.memset(v_aug[:, p, :, :, HD], 1.0).then_inc(padded, 1)
            pool.memset(spare[:], 0.0).then_inc(stored, 16)
            pool.wait_ge(tables_loaded, TABLES)

            def at_beat(frame, beat):
                for b, _ in due(ADD_BO, beat, frame):
                    add_bo(b)
                for b, k in due(CUT, beat, frame):
                    cut_pair(b, k)
                for b, t in due(ROTATE, beat, frame):
                    rotate(b, t)
                for b, _ in due(ROOT1, beat, frame):
                    inverse_root((ln1_step, b.n * LN1 + LN1), rstd1_ready, var1, rstd1)
                for b, _ in due(ROOT2, beat, frame, of_pair=True):
                    inverse_root((ln2_step, b.pair * LN2 + LN2), rstd2_ready, var2, rstd2)
                for b, i in due(SCALE_HIDDEN, beat, frame, of_pair=True):
                    scale_hidden(b, i)

            schedule(pool, at_beat)


def kernel(**inputs):
    import concourse.bacc as bacc
    from concourse.bass_utils import run_bass_kernel_spmd

    f32 = np.float32
    inv_freq = (f32(1.0) / f32(10000.0) ** (np.arange(0, HD, 2, dtype=f32) / f32(HD))).astype(f32)
    angle = np.arange(SEQ, dtype=f32)[:, None] * inv_freq[None, :]
    cos = np.repeat(np.cos(angle), 2, axis=1)
    sin = np.repeat(np.sin(angle), 2, axis=1)
    sin[:, 0::2] *= -1
    rope = np.stack([cos, sin]).reshape(2, TILES, P, HD).transpose(2, 0, 1, 3)
    mask = np.zeros((P, SEQ), f32)
    mask[:, P:] = np.where(np.arange(P)[None, :] > np.arange(P)[:, None], f32(MASKED), f32(0))
    tables = {"rope": rope, "mask": mask, "ident": np.eye(P, dtype=f32)}

    names = ["L0_attn_x", "L0_attn_wq", "L0_attn_bq", "L0_attn_wk", "L0_attn_bk", "L0_attn_wv", "L0_attn_bv",
             "L0_attn_wo", "L0_attn_bo", "L0_ffn_Wg", "L0_ffn_W1", "L0_ffn_b1", "L0_ffn_W2", "L0_ffn_b2"]
    nc = bacc.Bacc("TRN2", target_bir_lowering=False, num_devices=1)
    arrays, args = {}, []
    for name, a in [(n, inputs[n]) for n in names] + list(tables.items()):
        a = np.ascontiguousarray(a)
        arrays[f"in_{name}"] = a
        args.append(nc.dram_tensor(f"in_{name}", a.shape, mybir.dt.from_np(a.dtype), kind="ExternalInput").ap())
    out = nc.dram_tensor("out", (BATCHES, SEQ, D), F32, kind="ExternalOutput").ap()
    score_rows = nc.dram_tensor("score_rows", (EXPERTS, BATCHES, SEQ), F32, kind="Internal").ap()
    layer(nc, *args, score_rows, out)
    r = run_bass_kernel_spmd(nc, [arrays], core_ids=[0])
    return r.results[0]["out"]
```

```python
from contextlib import ExitStack

import numpy as np

import concourse.bass as bass
from concourse import mybir

F32 = mybir.dt.float32
F32R = mybir.dt.float32r
U32 = mybir.dt.uint32
ALU = mybir.AluOpType
ACT = mybir.ActivationFunctionType

P = 128
BATCHES, SEQ, D = 16, 256, 128
HEADS = 16
HD = D // HEADS
TILES = SEQ // P
ROWS = 32
GROUP = P // ROWS
GROUPS = HEADS // GROUP
MAX_ROW = 3 * HD
EXPERTS, HIDDEN = 8, 256
HT = HIDDEN // P
UNITS = EXPERTS * HT
PAIR = 2 * SEQ
HIDS = 4
EPS = 1e-5
SCALE = float(1.0 / np.sqrt(np.float32(HD)))
MASKED = -1e9 / SCALE
CAUSAL = SEQ + P
BANK = 512

FRAME = 128
LOAD = -226
ADD_BO = -23
TURN_X = -127
COPY_XT = -127
PROJECT = (-123, -108)
BIAS_QKV = (-121, -112)
ROTATE = (-83, -83)
SPLIT_QK = -82
TURN_QK = (-70, -62, -43, -18)
COPY_QK = (-70, -61, -43, -15)
MAXIMA = (-58, -55, -47, -41, -29, -24, -17, -9, -5, -1, 4, 15, 27, 36, 49, 62)
NEGATE_MAX = (-6, 70)
TURN_QUERIES = (-4, 72)
COPY_QUERIES = (-4, 76)
SCORES = (3, 6, 13, 27, 33, 42, 57, 67, 80, 83, 94, 104, 112, 120, 124, 128)
CUT = (59, 64, 71, 91, 111, 126, 160, 162)
TIMES_V = (68, 76, 129, 134)
COPY_O = (80, 148)
TURN_O = (155, 178)
NORMALISE = (155, 177)
TURN_ATTN = 193
COPY_ATTNT = 192
PROJECT_O = 203
RESIDUAL1 = 202
ROOT1 = 235
NORM1 = 219
TURN_X1 = 230
COPY_X1T = 230
ROUTE = 240
ROUTE_LOGITS = 250
ROUTE_EXP = 253
ROUTE_SCORES = 257
TURN_SCORE = 263
COPY_SCORET = 268
SAVE_SCORE = 220
SPLIT_X1 = 372
HIDDEN_PRODUCT = (380, 409, 425, 454, 466, 487, 491, 499, 505, 538, 544, 567, 582, 593, 606, 619)
RELU = (412, 436, 449, 458, 466, 495, 498, 507, 519, 532, 562, 576, 591, 596, 613, 629)
SCALE_HIDDEN = (457, 464, 485, 492, 498, 527, 535, 550, 558, 563, 609, 613, 623, 625, 626, 662)
HIDDEN_HIGH = (454, 460, 468, 483, 498, 518, 522, 541, 563, 582, 592, 613, 620, 634, 644, 648)
HIDDEN_LOW = (454, 468, 486, 490, 500, 525, 532, 542, 583, 594, 607, 615, 618, 635, 647, 665)
LOAD_SCORES = (363, 404, 415, 529)
OPEN_Y = 444
ADD_UNIT = (471, 471, 504, 510, 524, 552, 553, 573, 603, 611, 624, 631, 632, 656, 671, 676)
COPY_Y = 680
TURN_Y = 689
COPY_Z2 = 689
MOMENTS2 = 701
ROOT2 = 758
NORM2 = 763
STORE = 748
WARM = (-103, -88, -83, -83, -78, -75, -74, -68, -53, -13, -4, 27, 36, 40, 46, 48, 49, 63, 116, 121, 139, 147, 154, 159, 169, 170, 179, 190, 215, 228, 247, 265, 284, 285, 295, 302, 328, 337, 354, 356, 361, 372, 376, 378, 403, 415, 429, 431)
SPLIT_W = (2, 8, 20, 53)
assert WARM[-1] < OPEN_Y
PREPARED_BEFORE = sum(beat + FRAME < TURN_QUERIES[1] for beat in (TURN_X, *PROJECT, *TURN_QK))

EARLY_MAXIMA, EARLY_SCORES = 3, 2
PREP, DONE, RT, LN1 = 7, 7, 11, 5
LN2 = 9
TABLES = 16 * 13


class Batch:

    def __init__(self, pair, parity):
        self.pair, self.parity = pair, parity

    @property
    def n(self):
        return self.pair * 2 + self.parity

    def shift(self, k):
        m = self.parity + k
        return Batch(self.pair + m // 2, m % 2)

    @property
    def peeled(self):
        return isinstance(self.pair, int)

    def at_start(self, k=0):
        return self.peeled and self.n <= k


def due(steps, beat, frame, of_pair=False):
    for k, s in enumerate(steps if isinstance(steps, tuple) else (steps,)):
        if (s - beat) % FRAME == 0:
            b = frame.shift(-((s - beat) // FRAME))
            if (not b.peeled or 0 <= b.n < BATCHES) and not (of_pair and b.parity):
                yield b, k


def layer(nc, x, wq, bq, wk, bk, wv, bv, wo, bo, wg, w1, b1, w2, b2, rope, mask, ident, score_rows, out):
    with ExitStack() as ctx:
        def sb(name, shape, dt=F32):
            return ctx.enter_context(nc.sbuf_tensor(name, shape, dt))

        def bank(name):
            return ctx.enter_context(nc.psum_tensor(name, [P, BANK], F32))

        def sem(name):
            return ctx.enter_context(nc.semaphore(name))

        wqkv = sb("wqkv", [P, 3 * D])
        bqkv = sb("bqkv", [P, 3 * D])
        wo_sb = sb("wo_sb", [P, D])
        bo_sb = sb("bo_sb", [P, D])
        wg_sb = sb("wg_sb", [P, EXPERTS])
        w1_all = sb("w1_all", [P, UNITS, P])
        w1_low = sb("w1_low", [P, UNITS, P], F32R)
        w1_high = sb("w1_high", [P, UNITS, P], F32R)
        w2_all = sb("w2_all", [P, UNITS, D])
        w2_low = sb("w2_low", [P, UNITS, D], F32R)
        w2_high = sb("w2_high", [P, UNITS, D], F32R)
        b1_rows = sb("b1_rows", [UNITS, P])
        b1_cols = sb("b1_cols", [P, UNITS])
        b2_sb = sb("b2_sb", [EXPERTS, D])
        rope_sb = sb("rope_sb", [P, 2, TILES, HD])
        mask_sb = sb("mask_sb", [P, SEQ])
        ident_sb = sb("ident_sb", [P, P])
        ident_r = sb("ident_r", [P, P], F32R)
        iota = sb("iota", [P, EXPERTS])
        spare = sb("spare", [P, 1])
        exp_spare = sb("exp_spare", [P, 1])
        neg_half = sb("neg_half", [P, 2 * TILES])

        x_tok = sb("x_tok", [P, 2, TILES, D])
        x_bo = sb("x_bo", [P, 2, TILES, D])
        xT = sb("xT", [P, SEQ])
        qk = sb("qk", [P, TILES, 2 * HEADS, HD])
        rope_cos = sb("rope_cos", [P, TILES, 2 * HEADS, HD])
        rope_sin = sb("rope_sin", [P, TILES, 2 * HEADS, HD])
        rot = sb("rot", [P, 2, TILES, HEADS, HD])
        split = sb("split", [P, 2, 2, TILES, HEADS, ROWS])
        kT = sb("kT", [P, 2, GROUPS, SEQ], F32R)
        qT_max = sb("qT_max", [P, GROUPS, SEQ], F32R)
        qT = sb("qT", [P, GROUPS, SEQ], F32R)
        v_aug = sb("v_aug", [P, 2, TILES, HEADS, ROWS])
        junk = sb("junk", [P, 2, TILES, SEQ])
        row_max = sb("row_max", [P, TILES, HEADS])
        probs = sb("probs", [P, HEADS, CAUSAL])
        oT = sb("oT", [P, GROUPS, SEQ])
        recip = sb("recip", [P, TILES, HEADS])
        attn = sb("attn", [P, TILES, HEADS, HD])
        attnT = sb("attnT", [P, SEQ])
        z1 = sb("z1", [P, TILES, D])
        stats1 = sb("stats1", [P, TILES, 6])
        mv1 = sb("mv1", [P, TILES, 2])
        var1 = sb("var1", [P, TILES])
        rstd1 = sb("rstd1", [P, TILES])
        x1 = sb("x1", [P, TILES, D])
        x1T = sb("x1T", [P, 2, SEQ])
        x1T_high = sb("x1T_high", [P, PAIR], F32R)
        x1T_low = sb("x1T_low", [P, PAIR], F32R)
        logits = sb("logits", [P, TILES, EXPERTS])
        top_logits = sb("top_logits", [P, TILES, 8])
        neg_top = sb("neg_top", [P, TILES])
        expd = sb("expd", [P, TILES, EXPERTS])
        top = sb("top", [P, TILES, 8])
        top_at = sb("top_at", [P, TILES, 8], U32)
        top_atf = sb("top_atf", [P, TILES, 2])
        top_sum = sb("top_sum", [P, TILES])
        top_inv = sb("top_inv", [P, TILES])
        hot = sb("hot", [P, 2, TILES, EXPERTS])
        hot_sum = sb("hot_sum", [P, TILES, EXPERTS])
        score = sb("score", [P, TILES, EXPERTS])
        scoreT = sb("scoreT", [EXPERTS, 2, SEQ])
        score_all = sb("score_all", [P, EXPERTS, PAIR])
        hid = sb("hid", [P, HIDS, PAIR])
        hid_scaled = sb("hid_scaled", [P, 4, PAIR])
        hid_low = sb("hid_low", [P, 4, PAIR], F32R)
        hid_high = sb("hid_high", [P, 4, PAIR], F32R)
        yT = sb("yT", [P, PAIR])
        z2 = sb("z2", [P, 2 * TILES, D])
        stats2 = sb("stats2", [P, 2 * TILES, 6])
        mv2 = sb("mv2", [P, 2 * TILES, 2])
        var2 = sb("var2", [P, 2 * TILES])
        rstd2 = sb("rstd2", [P, 2 * TILES])
        out_tok = sb("out_tok", [P, 2 * TILES, D])

        ps_score = bank("ps_score")
        ps_max = bank("ps_max")
        ps_pv = bank("ps_pv")
        ps_hid = [bank("ps_hid0"), bank("ps_hid1")]
        ps_y = bank("ps_y")
        ps_prep = bank("ps_prep")
        ps_done = bank("ps_done")

        tables_loaded = sem("tables_loaded")
        w_loaded = sem("w_loaded")
        zeroed = sem("zeroed")
        padded = sem("padded")
        b1_turned = sem("b1_turned")
        setup_done = sem("setup_done")
        w_high = sem("w_high")
        w_split = sem("w_split")
        x_loaded = [sem("x_loaded0"), sem("x_loaded1")]
        x_bo_ready = sem("x_bo_ready")
        prep_full = sem("prep_full")
        prep_read = sem("prep_read")
        rope_terms = sem("rope_terms")
        roped = sem("roped")
        high_ready = sem("high_ready")
        split_ready = sem("split_ready")
        max_full = sem("max_full")
        max_read = sem("max_read")
        neg_max_ready = sem("neg_max_ready")
        qT_full = sem("qT_full")
        qT_read = sem("qT_read")
        scores_full = sem("scores_full")
        exp_done = sem("exp_done")
        cut = sem("cut")
        pv_full = sem("pv_full")
        pv_read = sem("pv_read")
        done_full = sem("done_full")
        done_read = sem("done_read")
        recip_ready = sem("recip_ready")
        ln1_step = sem("ln1_step")
        rstd1_ready = sem("rstd1_ready")
        x1_ready = sem("x1_ready")
        route_step = sem("route_step")
        scored = sem("scored")
        route_exp = sem("route_exp")
        score_saved = [sem("score_saved0"), sem("score_saved1")]
        score_loaded = [sem(f"score_loaded{k}") for k in range(len(LOAD_SCORES))]
        x1_high_ready = sem("x1_high_ready")
        x1_split = sem("x1_split")
        hid_full = sem("hid_full")
        hid_ready = sem("hid_ready")
        hid_scaled_ready = sem("hid_scaled_ready")
        hid_high_ready = sem("hid_high_ready")
        hid_split = sem("hid_split")
        unit_added = sem("unit_added")
        y_read = sem("y_read")
        emit_full = sem("emit_full")
        emit_read = sem("emit_read")
        ln2_step = sem("ln2_step")
        rstd2_ready = sem("rstd2_ready")
        out_ready = sem("out_ready")
        stored = sem("stored")

        def schedule(eng, at_beat):
            def frame(b):
                for beat in range(FRAME):
                    at_beat(b, beat)

            for n in range(-1, 4):
                frame(Batch(n // 2, n % 2))
            with eng.Fori(2, BATCHES // 2 - 1) as pair:
                for parity in range(2):
                    frame(Batch(pair, parity))
            for n in range(BATCHES - 2, BATCHES + 4):
                frame(Batch(n // 2, n % 2))

        def score_bank(b, h, bank_):
            if b.at_start((EARLY_MAXIMA if bank_ is ps_max else EARLY_SCORES) - 1):
                return (ps_hid[bank_ is ps_max] if h % 2 else bank_), 2
            return bank_, 1

        def value(eng, count):
            return count if isinstance(count, int) else eng.to_reg(count)

        def wait_apart(eng, semaphore, count):
            count = value(eng, count)
            eng.wait_ge(tables_loaded, TABLES)
            eng.wait_ge(semaphore, count)

        block = ctx.enter_context(nc.Block())

        @block.sync
        def _(sp):
            def load(b):
                src = x[bass.ds(b.n, 1)].rearrange("a (t p) d -> p (a t) d", p=P)
                sp.dma_start(x_tok[:, b.parity], src).then_inc(x_loaded[b.parity], 16)

            def save_score(b):
                sp.wait_ge(done_read, b.n * DONE + DONE)
                sp.dma_start(score_rows[:, bass.ds(b.n, 1), :], scoreT[:, b.parity:b.parity + 1, :]
                             ).then_inc(score_saved[b.parity], 16)

            def load_scores(b, k):
                n, parts = EXPERTS // len(LOAD_SCORES), UNITS // len(LOAD_SCORES)
                saved, used = value(sp, b.pair * 16 + 16), value(sp, b.pair * UNITS - UNITS + (k + 1) * parts)
                if k == 0:
                    for s in score_saved:
                        sp.wait_ge(s, saved)
                if not b.at_start():
                    sp.wait_ge(hid_scaled_ready, used)
                src = score_rows[k * n:(k + 1) * n, bass.ds(b.n, 2), :].rearrange("e b s -> e (b s)")
                sp.dma_start(score_all[:, k * n:(k + 1) * n, :], src.partition_broadcast(P)
                             ).then_inc(score_loaded[k], 16)

            def store(b):
                sp.wait_ge(out_ready, b.pair * 2 * TILES + 2 * TILES)
                dst = out[bass.ds(b.n, 2)].rearrange("a (t p) d -> p (a t) d", p=P)
                sp.dma_start(dst, out_tok[:]).then_inc(stored, 16)

            load(Batch(0, 0))
            for i, (w, b) in enumerate(((wq, bq), (wk, bk), (wv, bv))):
                sp.dma_start(wqkv[:, i * D:(i + 1) * D], w).then_inc(tables_loaded, 16)
                sp.dma_start(bqkv[:, i * D:(i + 1) * D], b.partition_broadcast(P)).then_inc(tables_loaded, 16)
            sp.dma_start(ident_sb[:], ident).then_inc(tables_loaded, 16)
            sp.dma_start(rope_sb[:], rope).then_inc(tables_loaded, 16)
            sp.dma_start(mask_sb[:], mask).then_inc(tables_loaded, 16)
            sp.dma_start(bo_sb[:], bo.partition_broadcast(P)).then_inc(tables_loaded, 16)
            sp.dma_start(wo_sb[:], wo).then_inc(tables_loaded, 16)
            sp.dma_start(wg_sb[:], wg).then_inc(tables_loaded, 16)
            sp.dma_start(b1_rows[:], b1.rearrange("e (t p) -> (e t) p", p=P)).then_inc(tables_loaded, 16)
            load(Batch(0, 1))
            sp.dma_start(w1_all[:].rearrange("p (e t) q -> p e (t q)", t=HT), w1.rearrange("e d h -> d e h")).then_inc(w_loaded, 16)
            sp.dma_start(w2_all[:], w2.rearrange("e (t p) d -> p (e t) d", p=P)).then_inc(w_loaded, 16)
            sp.dma_start(b2_sb[:], b2).then_inc(w_loaded, 16)

            def at_beat(frame, beat):
                for b, _ in due(LOAD, beat, frame):
                    if not b.at_start(1):
                        turned, added = value(sp, (b.n - 2) * PREP + 1), value(sp, b.n - 1)
                        sp.wait_ge(prep_full, turned)
                        sp.wait_ge(x_bo_ready, added)
                        load(b)
                for b, _ in due(SAVE_SCORE, beat, frame):
                    save_score(b)
                for b, k in due(LOAD_SCORES, beat, frame, of_pair=True):
                    load_scores(b, k)
                for b, _ in due(STORE, beat, frame, of_pair=True):
                    store(b)

            schedule(sp, at_beat)
            sp.wait_ge(stored, 16 + 16 * BATCHES // 2)

        @block.tensor
        def _(pe):
            def turn(dst, src, n=P):
                return pe.transpose(dst, src, ident_sb[:n, :n])

            def prep_fill(b, k):
                if k:
                    pe.wait_ge(prep_read, b.n * PREP + k)
                if not b.at_start():
                    if k == PREPARED_BEFORE:
                        pe.wait_ge(qT_read, b.n * 2)
                    elif k == 0:
                        pe.wait_ge(qT_read, b.n * 2 - 1)

            def turn_x(b):
                prep_fill(b, 0)
                pe.wait_ge(x_loaded[b.parity], b.pair * 16 + 16)
                for t in range(TILES):
                    last = turn(ps_prep[:, t * P:(t + 1) * P], x_tok[:, b.parity, t, :])
                last.then_inc(prep_full, 1)

            def project(b, t):
                prep_fill(b, 1 + t)
                pe.matmul(ps_prep[:, 0:3 * D], xT[:, t * P:(t + 1) * P], wqkv[:], start=True,
                          stop=True).then_inc(prep_full, 1)

            def turn_split(b, which, half):
                for g in range(2):
                    for t in range(TILES):
                        src = split[:, b.parity, which, t, (2 * half + g) * GROUP:(2 * half + g + 1) * GROUP, :]
                        last = turn(ps_prep[:, g * SEQ + t * P:g * SEQ + (t + 1) * P],
                                    src.rearrange("p h r -> p (h r)"))
                return last

            def turn_qk(b, i):
                prep_fill(b, 3 + i)
                if i == 0:
                    pe.wait_ge(split_ready, b.n * 2 + 2)
                turn_split(b, 1 - i % 2, i // 2).then_inc(prep_full, 1)

            def turn_queries(b, half):
                pe.wait_ge(neg_max_ready, b.n * 2 + half + 1)
                if half == 0:
                    pe.wait_ge(prep_read, b.n * PREP + PREP)
                    if PREPARED_BEFORE == PREP and not b.at_start():
                        pe.wait_ge(qT_read, b.n * 2)
                else:
                    last = b.peeled and b.n == BATCHES - 1
                    pe.wait_ge(prep_read, b.n * PREP + PREP + (0 if last else PREPARED_BEFORE))
                    if PREPARED_BEFORE == 0 or last:
                        pe.wait_ge(qT_read, b.n * 2 + 1)
                turn_split(b, 0, half).then_inc(qT_full, 1)

            def max_scores(b, h):
                g, r = h // GROUP, h % GROUP * ROWS
                bank_, ago = score_bank(b, h, ps_max)
                if h >= ago or not b.at_start():
                    pe.wait_ge(max_read, b.n * HEADS + h - ago + 1)
                if h % (HEADS // 2) == 0:
                    pe.wait_ge(prep_read, b.n * PREP + 5 + h // (HEADS // 2) * 2)
                for t in range(TILES):
                    last = pe.matmul(bank_[:, t * SEQ:(t + 1) * SEQ],
                                     qT_max[r:r + MAX_ROW, g, t * P:(t + 1) * P],
                                     kT[r:r + MAX_ROW, b.parity, g, :], start=True, stop=True)
                last.then_inc(max_full, 1)

            def scores(b, h):
                g, r = h // GROUP, h % GROUP * ROWS
                if h % (HEADS // 2) == 0:
                    pe.wait_ge(qT_read, b.n * 2 + 1 + h // (HEADS // 2))
                bank_, ago = score_bank(b, h, ps_score)
                if h >= ago or not b.at_start():
                    pe.wait_ge(exp_done, b.n * HEADS + h - ago + 1)
                for i, t in enumerate(reversed(range(TILES))):
                    last = pe.matmul(bank_[:, i * SEQ:(i + 1) * SEQ],
                                     kT[r:r + ROWS, b.parity, g, t * P:(t + 1) * P],
                                     qT[r:r + ROWS, g, :], start=True, stop=True)
                last.then_inc(scores_full, 1)

            def times_v(b, g):
                pe.wait_ge(cut, b.n * (HEADS // 2) + 2 * g + 2)
                if g == 2:
                    pe.wait_ge(pv_read, b.n * 2 + 1)
                elif g == 0 and not b.at_start():
                    pe.wait_ge(pv_read, b.n * 2)
                for j in range(GROUP):
                    h, c = g * GROUP + j, g % 2 * SEQ
                    dst = ps_pv[j * ROWS:(j + 1) * ROWS, :]
                    pe.matmul(dst[:, c:c + SEQ], v_aug[:, b.parity, 0, h, :], probs[:, h, P:CAUSAL],
                              start=True, stop=False)
                    last = pe.matmul(dst[:, c + P:c + SEQ], v_aug[:, b.parity, 1, h, :], probs[:, h, 0:P],
                                     start=False, stop=True)
                if g % 2:
                    last.then_inc(pv_full, 1)

            def done_fill(b, k):
                if k:
                    pe.wait_ge(done_read, b.n * DONE + k)
                elif not b.at_start():
                    pe.wait_ge(done_read, b.n * DONE)

            def turn_o(b, t):
                done_fill(b, t)
                if t == 0:
                    pe.wait_ge(pv_read, b.n * 2 + 2)
                for g in range(GROUPS):
                    last = turn(ps_done[:, g * P:(g + 1) * P], oT[:, g, t * P:(t + 1) * P])
                last.then_inc(done_full, 1)

            def turn_attn(b):
                done_fill(b, 2)
                for t in range(TILES):
                    last = turn(ps_done[:, t * P:(t + 1) * P], attn[:, t].rearrange("p h d -> p (h d)"))
                last.then_inc(done_full, 1)

            def project_o(b):
                done_fill(b, 3)
                for t in range(TILES):
                    last = pe.matmul(ps_done[:, t * P:(t + 1) * P], attnT[:, t * P:(t + 1) * P], wo_sb[:],
                                     start=True, stop=True)
                last.then_inc(done_full, 1)

            def turn_x1(b):
                done_fill(b, 4)
                pe.wait_ge(x1_ready, b.n * TILES + TILES)
                for t in range(TILES):
                    last = turn(ps_done[:, t * P:(t + 1) * P], x1[:, t, :])
                last.then_inc(done_full, 1)

            def route(b):
                done_fill(b, 5)
                for t in range(TILES):
                    last = pe.matmul(ps_done[:, t * EXPERTS:(t + 1) * EXPERTS],
                                     x1T[:, b.parity, t * P:(t + 1) * P], wg_sb[:], start=True, stop=True)
                last.then_inc(done_full, 1)

            def turn_score(b):
                done_fill(b, 6)
                pe.wait_ge(scored, b.n * 2 + 2)
                for t in range(TILES):
                    last = turn(ps_done[0:EXPERTS, t * P:(t + 1) * P], score[:, t, :])
                last.then_inc(done_full, 1)

            def products(dst, w_high, w_low, rows_high, rows_low, start, stop):
                pe.matmul(dst, w_high, rows_high, start=start, stop=False)
                pe.matmul(dst, w_low, rows_high, start=False, stop=False)
                return pe.matmul(dst, w_high, rows_low, start=False, stop=stop)

            def hidden(b, i):
                if i == 0:
                    pe.wait_ge(x1_split, b.pair + 1)
                    if b.at_start():
                        pe.wait_ge(w_split, len(SPLIT_W))
                        pe.wait_ge(max_read, EARLY_MAXIMA * HEADS)
                        pe.wait_ge(exp_done, EARLY_SCORES * HEADS)
                if i >= 2 or not b.at_start():
                    pe.wait_ge(hid_ready, b.pair * UNITS + i - 1)
                products(ps_hid[i % 2][:], w1_high[:, i, :], w1_low[:, i, :], x1T_high[:], x1T_low[:],
                         True, True).then_inc(hid_full, 1)

            def open_y(b):
                pe.wait_ge(done_read, b.n * DONE + 2 * DONE)
                if not b.at_start():
                    pe.wait_ge(emit_read, b.pair)
                pe.matmul(ps_y[:], b2_sb[:], scoreT[:].rearrange("e b s -> e (b s)"), start=True, stop=False)
                for part in (x1T_high, x1T_low):
                    pe.matmul(ps_y[:], ident_r[:], part[:], start=False, stop=False)

            def add_unit(b, i):
                pe.wait_ge(hid_split, b.pair * UNITS + i + 1)
                products(ps_y[:], w2_high[:, i, :], w2_low[:, i, :], hid_high[:, i % 4, :],
                         hid_low[:, i % 4, :], False, i == UNITS - 1).then_inc(unit_added, 1)

            def turn_y(b):
                pe.wait_ge(y_read, b.pair + 1)
                for t in range(2 * TILES):
                    last = turn(ps_y[:, t * P:(t + 1) * P], yT[:, t * P:(t + 1) * P])
                last.then_inc(emit_full, 1)

            def keep_clock():
                pe.matmul(ps_y[:, 0:3 * D], ident_sb[:], wqkv[:], start=True, stop=True)

            pe.wait_ge(tables_loaded, TABLES)
            turn(ps_done[:, 0:UNITS], b1_rows[:], UNITS).then_inc(b1_turned, 1)
            pe.wait_ge(setup_done, 2)

            def at_beat(frame, beat):
                for b, h in due(SCORES, beat, frame):
                    scores(b, h)
                for b, h in due(MAXIMA, beat, frame):
                    max_scores(b, h)
                for b, half in due(TURN_QUERIES, beat, frame):
                    turn_queries(b, half)
                for b, _ in due(TURN_X, beat, frame):
                    turn_x(b)
                for b, t in due(PROJECT, beat, frame):
                    project(b, t)
                for b, i in due(TURN_QK, beat, frame):
                    turn_qk(b, i)
                for b, g in due(TIMES_V, beat, frame):
                    times_v(b, g)
                for b, i in due(HIDDEN_PRODUCT, beat, frame, of_pair=True):
                    hidden(b, i)
                for b, _ in due(WARM, beat, frame):
                    if b.peeled and b.n == 0:
                        keep_clock()
                for b, t in due(TURN_O, beat, frame):
                    turn_o(b, t)
                for b, _ in due(TURN_ATTN, beat, frame):
                    turn_attn(b)
                for b, _ in due(PROJECT_O, beat, frame):
                    project_o(b)
                for b, _ in due(TURN_X1, beat, frame):
                    turn_x1(b)
                for b, _ in due(ROUTE, beat, frame):
                    route(b)
                for b, _ in due(TURN_SCORE, beat, frame):
                    turn_score(b)
                for b, _ in due(TURN_Y, beat, frame, of_pair=True):
                    turn_y(b)
                for b, _ in due(OPEN_Y, beat, frame, of_pair=True):
                    open_y(b)
                for b, i in due(ADD_UNIT, beat, frame, of_pair=True):
                    add_unit(b, i)

            schedule(pe, at_beat)

        @block.scalar
        def _(act):
            def copy_xT(b):
                act.wait_ge(prep_full, b.n * PREP + 1)
                act.activation(xT[:], ps_prep[:, 0:SEQ], ACT.Copy).then_inc(prep_read, 1)

            def copy_qk(b, i):
                act.wait_ge(prep_full, b.n * PREP + 4 + i)
                act.activation(kT[:, b.parity, i:i + 2, :].rearrange("p g s -> p (g s)"), ps_prep[:], ACT.Copy
                               ).then_inc(prep_read, 1)

            def copy_queries(b, half):
                act.wait_ge(qT_full, b.n * 2 + half + 1)
                act.activation(qT[:, 2 * half:2 * half + 2, :].rearrange("p g s -> p (g s)"), ps_prep[:], ACT.Copy
                               ).then_inc(qT_read, 1)

            def exponent(b, h):
                act.wait_ge(scores_full, b.n * HEADS + h + 1)
                act.activation(probs[:, h, :], score_bank(b, h, ps_score)[0][:, P:P + CAUSAL], ACT.Exp,
                               scale=SCALE).then_inc(exp_done, 1)

            def copy_o(b, half):
                act.wait_ge(pv_full, b.n * 2 + half + 1)
                act.activation(oT[:, 2 * half:2 * half + 2, :].rearrange("p g s -> p (g s)"), ps_pv[:],
                               ACT.Copy).then_inc(pv_read, 1)

            def copy_done(b, k, dst, n):
                act.wait_ge(done_full, b.n * DONE + k + 1)
                act.activation(dst, ps_done[:, 0:n], ACT.Copy).then_inc(done_read, 1)

            def route_exponent(b):
                act.wait_ge(route_step, b.n * RT + 3)
                for t in range(TILES):
                    act.activation(expd[:, t, :], logits[:, t, :], ACT.Exp,
                                   bias=neg_top[:, t:t + 1]).then_inc(route_exp, 1)

            def split_w(k):
                act.wait_ge(w_loaded, 48)
                part = slice(k * UNITS // len(SPLIT_W), (k + 1) * UNITS // len(SPLIT_W))
                act.activation(w1_high[:, part, :], w1_all[:, part, :], ACT.Copy)
                act.activation(w2_high[:, part, :], w2_all[:, part, :], ACT.Copy).then_inc(w_high, 1)

            def split_x1(b):
                if not b.at_start():
                    act.wait_ge(hid_full, b.pair * UNITS)
                act.wait_ge(done_read, b.n * DONE + DONE + 5)
                act.activation(x1T_high[:], x1T[:].rearrange("p b s -> p (b s)"), ACT.Copy
                               ).then_inc(x1_high_ready, 1)

            def relu(b, i):
                if i >= HIDS or not b.at_start():
                    act.wait_ge(hid_scaled_ready, b.pair * UNITS + i - HIDS + 1)
                act.wait_ge(hid_full, b.pair * UNITS + i + 1)
                act.activation(hid[:, i % HIDS, :], ps_hid[i % 2][:], ACT.Relu,
                               bias=b1_cols[:, i:i + 1]).then_inc(hid_ready, 1)

            def hidden_high(b, i):
                act.wait_ge(hid_scaled_ready, b.pair * UNITS + i + 1)
                act.activation(hid_high[:, i % 4, :], hid_scaled[:, i % 4, :], ACT.Copy
                               ).then_inc(hid_high_ready, 1)

            def copy_y(b):
                act.wait_ge(unit_added, b.pair * UNITS + UNITS)
                act.activation(yT[:], ps_y[:], ACT.Copy).then_inc(y_read, 1)

            def copy_z2(b):
                act.wait_ge(emit_full, b.pair + 1)
                if not b.at_start():
                    act.wait_ge(out_ready, b.pair * 2 * TILES)
                act.activation(z2[:].rearrange("p t d -> p (t d)"), ps_y[:], ACT.Copy
                               ).then_inc(emit_read, 1)

            act.wait_ge(padded, 1)
            act.activation(exp_spare[:], neg_half[:, 0:1], ACT.Exp)
            act.wait_ge(setup_done, 2)

            def at_beat(frame, beat):
                for b, h in due(SCORES, beat, frame):
                    exponent(b, h)
                for b, _ in due(COPY_XT, beat, frame):
                    copy_xT(b)
                for b, half in due(COPY_QUERIES, beat, frame):
                    copy_queries(b, half)
                for b, i in due(COPY_QK, beat, frame):
                    if i % 2 == 0:
                        copy_qk(b, i)
                for b, half in due(COPY_O, beat, frame):
                    copy_o(b, half)
                for b, _ in due(COPY_ATTNT, beat, frame):
                    copy_done(b, 2, attnT[:], SEQ)
                for b, _ in due(COPY_X1T, beat, frame):
                    copy_done(b, 4, x1T[:, b.parity, :], SEQ)
                for b, _ in due(ROUTE_EXP, beat, frame):
                    route_exponent(b)
                for b, _ in due(SPLIT_X1, beat, frame, of_pair=True):
                    split_x1(b)
                for b, i in due(HIDDEN_HIGH, beat, frame, of_pair=True):
                    hidden_high(b, i)
                for b, i in due(RELU, beat, frame, of_pair=True):
                    relu(b, i)
                for b, _ in due(COPY_Y, beat, frame, of_pair=True):
                    copy_y(b)
                for b, _ in due(COPY_Z2, beat, frame, of_pair=True):
                    copy_z2(b)
                for b, k in due(SPLIT_W, beat, frame):
                    if b.peeled and b.n == 1:
                        split_w(k)

            schedule(act, at_beat)

        @block.vector
        def _(dve):
            def bias_qkv(b, t):
                dve.wait_ge(prep_full, b.n * PREP + 2 + t)
                if not b.at_start():
                    dve.wait_ge(roped, b.n * TILES)
                if not b.at_start(1):
                    dve.wait_ge(pv_full, b.n * 2 - 2)
                dve.tensor_tensor(qk[:, t].rearrange("p h d -> p (h d)"), ps_prep[:, 0:2 * D],
                                  bqkv[:, 0:2 * D], ALU.add)
                dve.tensor_tensor(v_aug[:, b.parity, t, :, 0:HD],
                                  ps_prep[:, 2 * D:3 * D].rearrange("p (h d) -> p h d", d=HD),
                                  bqkv[:, 2 * D:3 * D].rearrange("p (h d) -> p h d", d=HD),
                                  ALU.add).then_inc(prep_read, 1)

            def slots(b, which, first, step, n):
                rows = split[:, b.parity, which].rearrange("p t h (s d) -> p (t h) s d", d=HD)
                return rows[:, :, first:first + step * (n - 1) + 1:step, :].bitcast(F32R)

            def split_qk(b):
                dve.wait_ge(roped, b.n * TILES + TILES)
                if not b.at_start(1):
                    dve.wait_ge(qT_full, b.n * 2 - 2)
                src = [rot[:, w].rearrange("p t h d -> p (t h) d") for w in range(2)]
                for w, step in ((0, 1), (1, 2)):
                    dve.tensor_copy(slots(b, w, 0, step, 2),
                                    src[w].unsqueeze(2).to_broadcast([P, TILES * HEADS, 2, HD])
                                    ).then_inc(high_ready, 1)
                for w, low in ((0, 2), (1, 1)):
                    dve.wait_ge(high_ready, b.n * 2 + w + 1)
                    dve.tensor_tensor(slots(b, w, low, 1, 1)[:, :, 0, :], src[w],
                                      slots(b, w, 0, 1, 1)[:, :, 0, :].bitcast(F32),
                                      ALU.subtract).then_inc(split_ready, 1)

            def copy_qk(b, i):
                dve.wait_ge(prep_full, b.n * PREP + 4 + i)
                dve.tensor_copy(qT_max[:, i - 1:i + 1, :].rearrange("p g s -> p (g s)"), ps_prep[:]
                                ).then_inc(prep_read, 1)

            def take_max(b, h):
                wait_apart(dve, max_full, b.n * HEADS + h + 1)
                for t in range(TILES):
                    n = (t + 1) * P
                    last = dve.tensor_tensor_reduce(
                        out=junk[:, h % 2, t, 0:n], in0=score_bank(b, h, ps_max)[0][:, t * SEQ:t * SEQ + n],
                        in1=mask_sb[:, SEQ - n:SEQ], scale=1.0, scalar=-3.0e38, op0=ALU.add, op1=ALU.max,
                        accum_out=row_max[:, t, h:h + 1])
                last.then_inc(max_read, 1)

            def negate_max(b, half):
                n = HEADS // 2
                dve.wait_ge(max_read, b.n * HEADS + (half + 1) * n)
                dve.tensor_scalar(split[:, b.parity, 0, :, half * n:(half + 1) * n, MAX_ROW].bitcast(F32R),
                                  row_max[:, :, half * n:(half + 1) * n], -1.0, None,
                                  ALU.mult).then_inc(neg_max_ready, 1)

            def normalise(b, t):
                dve.wait_ge(done_full, b.n * DONE + t + 1)
                o = ps_done[:].rearrange("p (h r) -> p h r", r=ROWS)
                dve.reciprocal(recip[:, t, :], o[:, :, HD]).then_inc(recip_ready, 1)
                dve.wait_ge(recip_ready, b.n * TILES + t + 1)
                dve.tensor_tensor(attn[:, t], o[:, :, 0:HD],
                                  recip[:, t, :].unsqueeze(2).to_broadcast([P, HEADS, HD]),
                                  ALU.mult).then_inc(done_read, 1)

            def moments(n, tiles, z, stats, mv, var, step):
                for t in range(tiles):
                    dve.bn_stats(stats[:, t, :], z[:, t, :]).then_inc(step, 1)
                for t in range(tiles):
                    wait_apart(dve, step, n + t + 1)
                    dve.bn_aggr(mv[:, t, :], stats[:, t, :]).then_inc(step, 1)
                dve.wait_ge(step, n + 2 * tiles)
                dve.tensor_scalar(var[:], mv[:, :, 1], EPS, None, ALU.add).then_inc(step, 1)

            def residual1(b):
                dve.wait_ge(x_bo_ready, b.n + 1)
                dve.wait_ge(done_full, b.n * DONE + 4)
                dve.tensor_tensor(z1[:].rearrange("p t d -> p (t d)"), ps_done[:, 0:SEQ],
                                  x_bo[:, b.parity].rearrange("p t d -> p (t d)"), ALU.add).then_inc(done_read, 1)
                dve.wait_ge(done_read, b.n * DONE + 4)
                moments(b.n * LN1, TILES, z1, stats1, mv1, var1, ln1_step)

            def norm1(b):
                dve.wait_ge(rstd1_ready, b.n + 1)
                for t in range(TILES):
                    dve.tensor_scalar(x1[:, t, :], z1[:, t, :], mv1[:, t, 0:1], rstd1[:, t:t + 1],
                                      ALU.subtract, ALU.mult).then_inc(x1_ready, 1)

            def route_logits(b):
                dve.wait_ge(done_full, b.n * DONE + 6)
                dve.tensor_copy(logits[:].rearrange("p t e -> p (t e)"),
                                ps_done[:, 0:TILES * EXPERTS]).then_inc(done_read, 1)
                wait_apart(dve, done_read, b.n * DONE + 6)
                for t in range(TILES):
                    dve.max(top_logits[:, t, :], logits[:, t, :]).then_inc(route_step, 1)
                dve.wait_ge(route_step, b.n * RT + 2)
                dve.tensor_scalar(neg_top[:], top_logits[:, :, 0], -1.0, None, ALU.mult).then_inc(route_step, 1)

            def route_scores(b):
                def after(k):
                    dve.wait_ge(route_step, b.n * RT + k)

                wait_apart(dve, route_exp, b.n * TILES + TILES)
                for t in range(TILES):
                    dve.max(top[:, t, :], expd[:, t, :]).then_inc(route_step, 1)
                wait_apart(dve, route_step, b.n * RT + 5)
                for t in range(TILES):
                    dve.max_index(top_at[:, t, :], top[:, t, :], expd[:, t, :]).then_inc(route_step, 1)
                dve.tensor_tensor(top_sum[:], top[:, :, 0], top[:, :, 1], ALU.add).then_inc(route_step, 1)
                after(7)
                dve.tensor_copy(top_atf[:], top_at[:, :, 0:2]).then_inc(route_step, 1)
                after(8)
                dve.reciprocal(top_inv[:], top_sum[:]).then_inc(route_step, 1)
                after(9)
                for t in range(TILES):
                    for k in range(2):
                        last = dve.tensor_scalar(hot[:, k, t, :], iota[:], top_atf[:, t, k:k + 1],
                                                 top[:, t, k:k + 1], ALU.is_equal, ALU.mult)
                last.then_inc(route_step, 1)
                after(11)
                dve.tensor_tensor(hot_sum[:], hot[:, 0], hot[:, 1], ALU.add).then_inc(scored, 1)
                dve.wait_ge(scored, b.n * 2 + 1)
                dve.tensor_tensor(score[:], hot_sum[:], top_inv[:].unsqueeze(2).to_broadcast([P, TILES, EXPERTS]),
                                  ALU.mult).then_inc(scored, 1)

            def copy_scoreT(b):
                if not b.at_start(1):
                    dve.wait_ge(score_saved[b.parity], b.pair * 16)
                dve.wait_ge(done_full, b.n * DONE + 7)
                dve.tensor_copy(scoreT[:, b.parity, :], ps_done[0:EXPERTS, 0:SEQ]).then_inc(done_read, 1)

            def split_w(k):
                dve.wait_ge(w_high, k + 1)
                part = slice(k * UNITS // len(SPLIT_W), (k + 1) * UNITS // len(SPLIT_W))
                for low, every, high in ((w1_low, w1_all, w1_high), (w2_low, w2_all, w2_high)):
                    last = dve.tensor_tensor(low[:, part, :], every[:, part, :],
                                             high[:, part, :].bitcast(F32), ALU.subtract)
                last.then_inc(w_split, 1)

            def split_x1(b):
                dve.wait_ge(x1_high_ready, b.pair + 1)
                dve.tensor_tensor(x1T_low[:], x1T[:].rearrange("p b s -> p (b s)"), x1T_high[:].bitcast(F32),
                                  ALU.subtract).then_inc(x1_split, 1)

            def hidden_low(b, i):
                dve.wait_ge(hid_high_ready, b.pair * UNITS + i + 1)
                dve.tensor_tensor(hid_low[:, i % 4, :], hid_scaled[:, i % 4, :],
                                  hid_high[:, i % 4, :].bitcast(F32), ALU.subtract).then_inc(hid_split, 1)

            def moments2(b):
                dve.wait_ge(emit_read, b.pair + 1)
                moments(b.pair * LN2, 2 * TILES, z2, stats2, mv2, var2, ln2_step)

            def norm2(b):
                dve.wait_ge(stored, b.pair * 16 + 16)
                dve.wait_ge(rstd2_ready, b.pair + 1)
                for t in range(2 * TILES):
                    dve.tensor_scalar(out_tok[:, t, :], z2[:, t, :], mv2[:, t, 0:1], rstd2[:, t:t + 1],
                                      ALU.subtract, ALU.mult).then_inc(out_ready, 1)

            dve.wait_ge(b1_turned, 1)
            dve.tensor_copy(b1_cols[:], ps_done[:, 0:UNITS]).then_inc(setup_done, 1)
            dve.wait_ge(tables_loaded, TABLES)
            dve.tensor_copy(ident_r[:], ident_sb[:]).then_inc(setup_done, 1)
            dve.wait_ge(padded, 5)

            def at_beat(frame, beat):
                for b, half in due(NEGATE_MAX, beat, frame):
                    negate_max(b, half)
                for b, h in due(MAXIMA, beat, frame):
                    take_max(b, h)
                for b, t in due(BIAS_QKV, beat, frame):
                    bias_qkv(b, t)
                for b, _ in due(SPLIT_QK, beat, frame):
                    split_qk(b)
                for b, i in due(COPY_QK, beat, frame):
                    if i % 2:
                        copy_qk(b, i)
                for b, t in due(NORMALISE, beat, frame):
                    normalise(b, t)
                for b, _ in due(RESIDUAL1, beat, frame):
                    residual1(b)
                for b, _ in due(NORM1, beat, frame):
                    norm1(b)
                for b, _ in due(ROUTE_LOGITS, beat, frame):
                    route_logits(b)
                for b, _ in due(ROUTE_SCORES, beat, frame):
                    route_scores(b)
                for b, _ in due(COPY_SCORET, beat, frame):
                    copy_scoreT(b)
                for b, _ in due(SPLIT_X1, beat, frame, of_pair=True):
                    split_x1(b)
                for b, i in due(HIDDEN_LOW, beat, frame, of_pair=True):
                    hidden_low(b, i)
                for b, _ in due(MOMENTS2, beat, frame, of_pair=True):
                    moments2(b)
                for b, _ in due(NORM2, beat, frame, of_pair=True):
                    norm2(b)
                for b, k in due(SPLIT_W, beat, frame):
                    if b.peeled and b.n == 1:
                        split_w(k)

            schedule(dve, at_beat)

        @block.gpsimd
        def _(pool):
            def add_bo(b):
                pool.wait_ge(x_loaded[b.parity], b.pair * 16 + 16)
                if not b.at_start(1):
                    pool.wait_ge(done_read, b.n * DONE - 2 * DONE + 4)
                for t in range(TILES):
                    last = pool.tensor_tensor(x_bo[:, b.parity, t, :], x_tok[:, b.parity, t, :], bo_sb[:], ALU.add)
                last.then_inc(x_bo_ready, 1)

            def rotate(b, t):
                pool.wait_ge(prep_read, b.n * PREP + 2 + t)
                if t == 0 and not b.at_start():
                    pool.wait_ge(split_ready, b.n * 2)
                table = [rope_sb[:, i, t].unsqueeze(1).to_broadcast([P, 2 * HEADS, HD]) for i in range(2)]
                pool.tensor_tensor(rope_cos[:, t], qk[:, t], table[0], ALU.mult).then_inc(rope_terms, 1)
                pairs = [a.rearrange("p h (c two) -> p h c two", two=2) for a in (rope_sin[:, t], qk[:, t], table[1])]
                for i in range(2):
                    last = pool.tensor_tensor(pairs[0][:, :, :, i], pairs[1][:, :, :, 1 - i], pairs[2][:, :, :, i],
                                              ALU.mult)
                last.then_inc(rope_terms, 1)
                pool.wait_ge(rope_terms, b.n * 2 * TILES + 2 * t + 2)
                pool.tensor_tensor(rot[:, :, t], rope_cos[:, t].rearrange("p (w h) d -> p w (h d)", w=2),
                                   rope_sin[:, t].rearrange("p (w h) d -> p w (h d)", w=2),
                                   ALU.add).then_inc(roped, 1)

            def cut_pair(b, k):
                wait_apart(pool, exp_done, b.n * HEADS + 2 * k + 2)
                block_ = probs[:, 2 * k:2 * k + 2, 0:2 * P].rearrange("p h (t q) -> p h t q", q=P)
                pool.affine_select(out=block_, in_=block_, compare_op=ALU.is_ge, fill=0.0, base=0,
                                   pattern=[[0, 2], [0, 2], [1, P]], channel_multiplier=-1).then_inc(cut, 1)

            def scale_hidden(b, i):
                part = UNITS // len(LOAD_SCORES)
                if i % part == 0:
                    pool.wait_ge(score_loaded[i // part], b.pair * 16 + 16)
                if i >= 4 or not b.at_start():
                    pool.wait_ge(unit_added, b.pair * UNITS + i - 3)
                pool.wait_ge(hid_ready, b.pair * UNITS + i + 1)
                pool.tensor_tensor(hid_scaled[:, i % 4, :], hid[:, i % HIDS, :], score_all[:, i // HT, :],
                                   ALU.mult).then_inc(hid_scaled_ready, 1)

            def inverse_root(variance_ready, rstd_ready, var, rstd):
                semaphore, count = variance_ready
                pool.wait_ge(semaphore, count)
                pool.tensor_tensor(rstd[:], var[:], neg_half[:, 0:rstd.shape[1]], ALU.pow).then_inc(rstd_ready, 1)

            pool.memset(neg_half[:], -0.5).then_inc(padded, 1)
            for t in (split, v_aug):
                pool.memset(t[:], 0.0).then_inc(zeroed, 1)
            pool.iota(iota[:], pattern=[[1, EXPERTS]], base=0, channel_multiplier=0,
                      allow_small_or_imprecise_dtypes=True).then_inc(padded, 1)
            pool.wait_ge(zeroed, 2)
            pool.memset(split[:, :, 1, :, :, MAX_ROW], 1.0).then_inc(padded, 1)
            for p in range(2):
                pool.memset(v_aug[:, p, :, :, HD], 1.0).then_inc(padded, 1)
            pool.memset(spare[:], 0.0).then_inc(stored, 16)
            pool.wait_ge(tables_loaded, TABLES)

            def at_beat(frame, beat):
                for b, _ in due(ADD_BO, beat, frame):
                    add_bo(b)
                for b, k in due(CUT, beat, frame):
                    cut_pair(b, k)
                for b, t in due(ROTATE, beat, frame):
                    rotate(b, t)
                for b, _ in due(ROOT1, beat, frame):
                    inverse_root((ln1_step, b.n * LN1 + LN1), rstd1_ready, var1, rstd1)
                for b, _ in due(ROOT2, beat, frame, of_pair=True):
                    inverse_root((ln2_step, b.pair * LN2 + LN2), rstd2_ready, var2, rstd2)
                for b, i in due(SCALE_HIDDEN, beat, frame, of_pair=True):
                    scale_hidden(b, i)

            schedule(pool, at_beat)


def kernel(**inputs):
    import concourse.bacc as bacc
    from concourse.bass_utils import run_bass_kernel_spmd

    f32 = np.float32
    inv_freq = (f32(1.0) / f32(10000.0) ** (np.arange(0, HD, 2, dtype=f32) / f32(HD))).astype(f32)
    angle = np.arange(SEQ, dtype=f32)[:, None] * inv_freq[None, :]
    cos = np.repeat(np.cos(angle), 2, axis=1)
    sin = np.repeat(np.sin(angle), 2, axis=1)
    sin[:, 0::2] *= -1
    rope = np.stack([cos, sin]).reshape(2, TILES, P, HD).transpose(2, 0, 1, 3)
    mask = np.zeros((P, SEQ), f32)
    mask[:, P:] = np.where(np.arange(P)[None, :] > np.arange(P)[:, None], f32(MASKED), f32(0))
    tables = {"rope": rope, "mask": mask, "ident": np.eye(P, dtype=f32)}

    names = ["L0_attn_x", "L0_attn_wq", "L0_attn_bq", "L0_attn_wk", "L0_attn_bk", "L0_attn_wv", "L0_attn_bv",
             "L0_attn_wo", "L0_attn_bo", "L0_ffn_Wg", "L0_ffn_W1", "L0_ffn_b1", "L0_ffn_W2", "L0_ffn_b2"]
    nc = bacc.Bacc("TRN2", target_bir_lowering=False, num_devices=1)
    arrays, args = {}, []
    for name, a in [(n, inputs[n]) for n in names] + list(tables.items()):
        a = np.ascontiguousarray(a)
        arrays[f"in_{name}"] = a
        args.append(nc.dram_tensor(f"in_{name}", a.shape, mybir.dt.from_np(a.dtype), kind="ExternalInput").ap())
    out = nc.dram_tensor("out", (BATCHES, SEQ, D), F32, kind="ExternalOutput").ap()
    score_rows = nc.dram_tensor("score_rows", (EXPERTS, BATCHES, SEQ), F32, kind="Internal").ap()
    layer(nc, *args, score_rows, out)
    r = run_bass_kernel_spmd(nc, [arrays], core_ids=[0])
    return r.results[0]["out"]
```
